# Optimizing a Trainium2 kernel written in Bass

```python
import numpy as np
import jax
import jax.numpy as jnp

def _softmax(x, axis=-1):
    return jax.nn.softmax(x, axis=axis)

def _gelu(x):
    return jax.nn.gelu(x, approximate=True)

def _silu(x):
    return jax.nn.silu(x)

def _sigmoid(x):
    return jax.nn.sigmoid(x)

def _layernorm(x, axis=-1, eps=1e-05):
    m = jnp.mean(x, axis=axis, keepdims=True)
    v = jnp.var(x, axis=axis, keepdims=True)
    return (x - m) / jnp.sqrt(v + eps)

def _scatter_add(tgt, idx, src, axis=0):
    return tgt.at[idx].add(src)

def _segment_sum(src, seg, n):
    return jax.ops.segment_sum(src, seg, n)
kernel_name = 'mk_prb_d1_jaxref_r8_c88366'

def setup_inputs(seed: int=0):
    np.random.seed(seed)
    _w = jnp.asarray

    def _L0_attn_setup():
        import jax, jax.numpy as jnp
        import numpy as np
        import math
        H = 128
        S = 16
        K = 4
        INNER = 2 * H
        BATCH, L = (2, 512)

        def _linrec_combine(c1, c2):
            a1, b1 = c1
            a2, b2 = c2
            return (a1 * a2, a2 * b1 + b2)
        key = jax.random.key(seed)
        ks = jax.random.split(key, 8)
        x = jax.random.normal(ks[0], (BATCH, L, H), dtype=jnp.float32)
        W_in = jax.random.normal(ks[1], (2 * INNER, H), dtype=jnp.float32) * 0.02
        conv_w = jax.random.normal(ks[2], (INNER, 1, K), dtype=jnp.float32) * 0.1
        conv_b = jnp.zeros((INNER,), dtype=jnp.float32)
        W_x = jax.random.normal(ks[3], (2 * S + INNER, INNER), dtype=jnp.float32) * 0.02
        W_dt = jax.random.normal(ks[4], (INNER, INNER), dtype=jnp.float32) * 0.02
        u = jax.random.uniform(ks[5], (INNER,), dtype=jnp.float32)
        b_dt = jnp.exp(u * (math.log(0.1) - math.log(0.001)) + math.log(0.001))
        A_log = jnp.log(jnp.broadcast_to(jnp.arange(1, S + 1, dtype=jnp.float32), (INNER, S)))
        D = jnp.ones((INNER,), dtype=jnp.float32)
        W_out = jax.random.normal(ks[6], (H, INNER), dtype=jnp.float32) * 0.02
        return {'x': x, 'W_in': W_in, 'conv_w': conv_w, 'conv_b': conv_b, 'W_x': W_x, 'W_dt': W_dt, 'b_dt': b_dt, 'A_log': A_log, 'D': D, 'W_out': W_out}
    _L0_attn_in = _L0_attn_setup()

    def _L0_ffn_setup():
        import jax, jax.numpy as jnp
        import numpy as np
        B, S, D = (4, 256, 128)
        E, H, TOP_K = (8, 256, 2)
        key = jax.random.key(seed)
        k_x, k_g, k_w1, k_w2, k_w3 = jax.random.split(key, 5)
        s_d = 1.0 / np.sqrt(D)
        s_h = 1.0 / np.sqrt(H)
        return {'x': jax.random.normal(k_x, (B, S, D), dtype=jnp.float32), 'w_gate': jax.random.normal(k_g, (D, E), dtype=jnp.float32) * s_d, 'w1': jax.random.normal(k_w1, (E, D, H), dtype=jnp.float32) * s_d, 'w3': jax.random.normal(k_w3, (E, D, H), dtype=jnp.float32) * s_d, 'w2': jax.random.normal(k_w2, (E, H, D), dtype=jnp.float32) * s_h}
    _L0_ffn_in = _L0_ffn_setup()
    _d = {'L0_attn_x': _L0_attn_in['x'], 'L0_attn_W_in': _L0_attn_in['W_in'], 'L0_attn_conv_w': _L0_attn_in['conv_w'], 'L0_attn_conv_b': _L0_attn_in['conv_b'], 'L0_attn_W_x': _L0_attn_in['W_x'], 'L0_attn_W_dt': _L0_attn_in['W_dt'], 'L0_attn_b_dt': _L0_attn_in['b_dt'], 'L0_attn_A_log': _L0_attn_in['A_log'], 'L0_attn_D': _L0_attn_in['D'], 'L0_attn_W_out': _L0_attn_in['W_out'], 'L0_ffn_w_gate': _L0_ffn_in['w_gate'], 'L0_ffn_w1': _L0_ffn_in['w1'], 'L0_ffn_w3': _L0_ffn_in['w3'], 'L0_ffn_w2': _L0_ffn_in['w2']}
    _x0 = _d['L0_attn_x']
    _d['L0_attn_x'] = jax.random.normal(jax.random.fold_in(jax.random.key(seed), 1), (32, 256, 128), dtype=_x0.dtype)
    del _x0
    return _d

def reference(L0_attn_x, L0_attn_W_in, L0_attn_conv_w, L0_attn_conv_b, L0_attn_W_x, L0_attn_W_dt, L0_attn_b_dt, L0_attn_A_log, L0_attn_D, L0_attn_W_out, L0_ffn_w_gate, L0_ffn_w1, L0_ffn_w3, L0_ffn_w2):

    def _L0_attn_ref(x, W_in, conv_w, conv_b, W_x, W_dt, b_dt, A_log, D, W_out):
        import jax, jax.numpy as jnp
        import numpy as np
        import math
        H = 128
        S = 16
        K = 4
        INNER = 2 * H
        BATCH, L = (2, 512)

        def _linrec_combine(c1, c2):
            a1, b1 = c1
            a2, b2 = c2
            return (a1 * a2, a2 * b1 + b2)
        xz = jnp.einsum('blh,ih->bli', x, W_in)
        x_proj, z = jnp.split(xz, 2, axis=-1)
        xc = jnp.transpose(x_proj, (0, 2, 1))
        xc = jax.lax.conv_general_dilated(xc, conv_w, window_strides=(1,), padding=[(K - 1, 0)], dimension_numbers=('NCH', 'OIH', 'NCH'), feature_group_count=INNER)
        xc = xc + conv_b[None, :, None]
        x_conv = jax.nn.silu(jnp.transpose(xc, (0, 2, 1)))
        x_ssm = jnp.einsum('bli,oi->blo', x_conv, W_x)
        Bm = x_ssm[..., :S]
        Cm = x_ssm[..., S:2 * S]
        dt_in = x_ssm[..., 2 * S:]
        dt = jax.nn.softplus(jnp.einsum('bli,oi->blo', dt_in, W_dt) + b_dt)
        alpha = jax.nn.sigmoid(dt * 0.1)
        B_gate = jax.nn.sigmoid(jnp.mean(Bm, axis=-1, keepdims=True))
        gated = (1.0 - alpha) * B_gate * x_conv
        alpha_c = jnp.clip(alpha, 0.01, 0.99)
        _, h = jax.lax.associative_scan(_linrec_combine, (alpha_c, gated), axis=1)
        C_gate = jax.nn.sigmoid(jnp.mean(Cm, axis=-1, keepdims=True))
        y = h * C_gate + D * x_conv
        y = y * jax.nn.silu(z)
        out = jnp.einsum('bli,hi->blh', y, W_out)
        return out

    def _L0_ffn_ref(x, w_gate, w1, w3, w2):
        import jax, jax.numpy as jnp
        import numpy as np
        B, S, D = (4, 256, 128)
        E, H, TOP_K = (8, 256, 2)
        bsz, seq_len, embed_dim = x.shape
        xt = x.reshape(-1, embed_dim)
        T = xt.shape[0]
        logits = xt @ w_gate
        top_logits, sel = jax.lax.top_k(logits, TOP_K)
        probs = jax.nn.softmax(top_logits, axis=-1).astype(x.dtype)
        h = jax.nn.silu(jnp.einsum('td,edh->eth', xt, w1)) * jnp.einsum('td,edh->eth', xt, w3)
        y = jnp.einsum('eth,ehd->etd', h, w2)
        t_idx = jnp.arange(T)
        yk = y[sel.T, t_idx[None, :], :]
        out = jnp.einsum('ktd,tk->td', yk, probs)
        return out.reshape(bsz, seq_len, embed_dim)
    x = L0_attn_x
    xn = _layernorm(x, axis=-1)
    x = x + _L0_attn_ref(xn, L0_attn_W_in, L0_attn_conv_w, L0_attn_conv_b, L0_attn_W_x, L0_attn_W_dt, L0_attn_b_dt, L0_attn_A_log, L0_attn_D, L0_attn_W_out) + _L0_ffn_ref(xn, L0_ffn_w_gate, L0_ffn_w1, L0_ffn_w3, L0_ffn_w2)
    return x

_drawn_inputs = setup_inputs


def setup_inputs(seed=0):
    import zlib

    import numpy as np

    out = dict(_drawn_inputs(seed))
    spreads = {'L0_attn_conv_b': (0.0, 0.8), 'L0_attn_D': (1.0, 0.6)}
    factors = {'L0_attn_W_in': 8.0,
     'L0_attn_conv_w': 8.0,
     'L0_attn_W_x': 8.0,
     'L0_attn_W_dt': 8.0,
     'L0_attn_b_dt': 8.0,
     'L0_attn_W_out': 8.0}
    for name, (base, spread) in spreads.items():
        noise = np.random.default_rng([zlib.crc32(name.encode()), seed]).standard_normal(out[name].shape)
        drawn = base * np.exp(spread * noise) if base else spread * noise
        out[name] = jnp.asarray(drawn.astype(out[name].dtype))
    for name, factor in factors.items():
        out[name] = (out[name] * factor).astype(out[name].dtype)
    return out
```

```python
import concourse.bass as bass
from concourse import mybir
from contextlib import ExitStack

F32 = mybir.dt.float32
F32R = mybir.dt.float32r
I32 = mybir.dt.int32
U32 = mybir.dt.uint32
ALU = mybir.AluOpType
ACT = mybir.ActivationFunctionType
AX_X = mybir.AxisListType.X

P = 128
BATCH, SEQ, D = 32, 256, 128
TOKENS = BATCH * SEQ
TILES = TOKENS // P
GROUP = 512
GROUPS = TOKENS // GROUP
GT = GROUP // P
SPG = GROUP // SEQ
INNER, STATE, TAPS = 256, 16, 4
HALVES = INNER // P
EXPERTS, HID, TOP_K = 8, 256, 2
SLOTS = 512
PAIRS = TOKENS * TOP_K
MOE_TILES = (PAIRS + EXPERTS * (SLOTS - 1)) // SLOTS
EPS = 1e-5
QUARTERS = 4
QT = TILES // QUARTERS
HALF_GROUPS = GROUPS // 2
EXP_CAP = 40.0
SLOT3 = 3
ROWS = MOE_TILES * SLOTS
CHAIN = 8
FILL_ROWS = 13
FILLS = ROWS // P // FILL_ROWS


def block_kernel(nc, x, W_in, conv_w, conv_b, W_x, W_dt, b_dt, A_log, D_skip, W_out,
                 w_gate, w1, w3, w2, out):
    assert FILLS * FILL_ROWS * P == ROWS
    xs_dram = nc.dram_tensor("moe_in", (ROWS, D), F32, kind="Internal").ap()
    ys_dram = nc.dram_tensor("moe_out", (ROWS, D), F32, kind="Internal").ap()

    ctx = ExitStack()
    with ctx:
        def sb(name, shape, dt=F32):
            return ctx.enter_context(nc.sbuf_tensor(name, shape, dt))

        def pb(name):
            return ctx.enter_context(nc.psum_tensor(name, [P, 2 * GROUP], F32))

        def sem(name):
            return ctx.enter_context(nc.semaphore(name))

        xacc = sb("xacc", [P, TILES, D])
        xnT = sb("xnT", [P, TOKENS])
        xn = sb("xn", [P, TILES * D])
        WinT = sb("WinT", [P, 2 * INNER])
        Wc = sb("Wc", [P, HALVES, INNER])
        WgB = sb("WgB", [P, 4, P])
        WoT = sb("WoT", [P, HALVES, D])
        cw = sb("cw", [P, HALVES, TAPS])
        cb = sb("cb", [P, HALVES])
        bdt = sb("bdt", [P, HALVES])
        dsk = sb("dsk", [P, HALVES])
        dsk8 = sb("dsk8", [P, HALVES])
        wg = sb("wg", [P, EXPERTS])
        ident = sb("ident", [P, P])
        prob = sb("prob", [P, TOP_K, TILES])
        slot_u = sb("slot_u", [P, TOP_K, TILES], U32)
        eid_i = sb("eid_i", [P, MOE_TILES], I32)
        zrow = sb("zrow", [P, 1, D])

        acc = sb("acc", [P, HALVES, GROUP])
        xc = sb("xc", [P, SLOT3, HALVES, GROUP])
        sz = sb("sz", [P, SLOT3, HALVES, GROUP])
        ebuf = sb("ebuf", [P, HALVES, GROUP])
        th = sb("th", [P, HALVES, GROUP])
        al = sb("al", [P, HALVES, GROUP])
        gbuf = sb("gbuf", [P, HALVES, GROUP])
        hbuf = sb("hbuf", [P, HALVES, GROUP])
        ybuf = sb("ybuf", [P, HALVES, GROUP])
        y2 = sb("y2", [P, HALVES, GROUP])
        thg = sb("thg", [P, 2, GROUP])

        whi = sb("whi", [P, 2, 2 * HID], F32R)
        wlo = sb("wlo", [P, 2, 2 * HID], F32R)
        xhi = sb("xhi", [P, 2, SLOTS], F32R)
        xlo = sb("xlo", [P, 2, SLOTS], F32R)

        def in_xn(at, n):
            return xn[:, at:at + n]
        w13 = [in_xn(512 * b, 512) for b in range(2)]
        w2b = [in_xn(1024 + 256 * b, 256) for b in range(2)]
        xs = [in_xn(1536 + 512 * b, 512) for b in range(2)]
        sil = in_xn(2560, 1024)
        hid = [in_xn(3584 + 1024 * b, 1024) for b in range(2)]
        yo = [in_xn(5632 + 512 * b, 512) for b in range(2)]
        got = [in_xn(2048 * b, 2048).rearrange("p (g k j d) -> p g k j d", g=2, k=TOP_K, j=GT)
               for b in range(SLOT3)]

        def flat(t):
            return t.rearrange("p a b -> p (a b)")
        win_raw = flat(acc[:, :, :])[:, 0:512].rearrange("p (a b) -> p a b", a=4)
        wdt_raw = flat(acc[:, :, :])[:, 512:1024].rearrange("p (a b) -> p a b", a=2)
        wx_raw = flat(ebuf[:, :, :])[:, 0:512].rearrange("p (a b) -> p a b", a=2)
        wxB = ebuf[0:STATE, 1, 0:256]
        wxC = ebuf[0:STATE, 1, 256:512]
        wo_raw = flat(th[:, :, :])[:, 0:256]
        wdtT = flat(th[:, :, :])[:, 512:1024].rearrange("p (a b) -> p a b", a=2)
        inv16 = th[0:STATE, 0, 256:256 + P]
        ones_pp = flat(al[:, :, :])[:, 0:128]
        tri = flat(al[:, :, :])[:, 128:256]
        iot = flat(al[:, :, :])[:, 256:640].bitcast(I32)
        ones64 = flat(al[:, :, :])[:, 640:704]
        thr = flat(al[:, :, :])[:, 704:832].rearrange("p (e m) -> p e m", e=EXPERTS)
        rev = flat(al[:, :, :])[:, 832:840]
        tix = flat(al[:, :, :])[:, 840:840 + MOE_TILES]
        nte = flat(al[:, :, :])[:, 896:904]
        nti = flat(al[:, :, :])[:, 904:912]
        base = flat(al[:, :, :])[:, 912:920]
        eid_f = flat(al[:, :, :])[:, 920:920 + MOE_TILES]
        st = flat(gbuf[:, :, :])[:, 0:QT * 6].rearrange("p (j s) -> p j s", s=6)
        mv = flat(gbuf[:, :, :])[:, 128:128 + QT * 2].rearrange("p (j s) -> p j s", s=2)
        var = flat(gbuf[:, :, :])[:, 192:192 + QT]
        std = flat(gbuf[:, :, :])[:, 224:224 + QT]
        rst = flat(gbuf[:, :, :])[:, 256:256 + QT]
        nrt = flat(gbuf[:, :, :])[:, 288:288 + QT]

        def je(t):
            return t.rearrange("p (j e) -> p j e", e=EXPERTS)
        L = je(hbuf[:, 0, :])
        L2 = je(hbuf[:, 1, :])
        oh1 = je(ybuf[:, 0, :])
        oh2 = je(ybuf[:, 1, :])
        msk = je(y2[:, 0, :])
        tmp = je(y2[:, 1, :])
        tot = je(thg[:, 0, :])
        inc = je(thg[:, 1, :])
        m1 = gbuf[:, 1, 0:64]
        m2 = gbuf[:, 1, 64:128]
        c1 = gbuf[:, 1, 128:192]
        sf = gbuf[:, 1, 192:320].rearrange("p (k j) -> p k j", k=TOP_K)
        dlt = gbuf[:, 1, 320:384]
        den = gbuf[:, 1, 384:448]
        cmp_m = flat(xc[:, 0, :, :])[:, 0:EXPERTS * 16].rearrange("p (e m) -> p e m", e=EXPERTS)
        cmp_t = flat(xc[:, 0, :, :])[:, 128:128 + MOE_TILES * EXPERTS].rearrange("p (t e) -> p t e", e=EXPERTS)

        PA, PB, PC, PD = pb("PA"), pb("PB"), pb("PC"), pb("PD")

        s_x = sem("s_x")
        s_wld = sem("s_wld")
        s_zrow = sem("s_zrow")
        s_fill = sem("s_fill")
        s_cst = sem("s_cst")
        s_wtp = sem("s_wtp")
        s_wcp = sem("s_wcp")
        s_dve = sem("s_dve")
        s_var = sem("s_var")
        s_std = sem("s_std")
        s_xn = sem("s_xn")
        s_xt = sem("s_xt")
        s_xnT = sem("s_xnT")
        s_lg = sem("s_lg")
        s_msk = sem("s_msk")
        s_rk = sem("s_rk")
        s_dlt = sem("s_dlt")
        s_edl = sem("s_edl")
        s_slot = sem("s_slot")
        s_eid = sem("s_eid")
        s_scat = sem("s_scat")
        s_xp = sem("s_xp")
        s_z = sem("s_z")
        s_tap0 = sem("s_tap0")
        s_taps = sem("s_taps")
        s_cv = sem("s_cv")
        s_xc = sem("s_xc")
        s_sz = sem("s_sz")
        s_u = sem("s_u")
        s_g = sem("s_g")
        s_exp = sem("s_exp")
        s_cap = sem("s_cap")
        s_ln = sem("s_ln")
        s_dt = sem("s_dt")
        s_th = sem("s_th")
        s_al = sem("s_al")
        s_thg = sem("s_thg")
        s_ch = sem("s_ch")
        s_y2 = sem("s_y2")
        s_out = sem("s_out")
        s_add = sem("s_add")
        s_w13 = [sem(f"s_w13_{b}") for b in range(2)]
        s_w2 = [sem(f"s_w2_{b}") for b in range(2)]
        s_xs = [sem(f"s_xs_{b}") for b in range(2)]
        s_ys = [sem(f"s_ys_{b}") for b in range(2)]
        s_whi = sem("s_whi")
        s_wlo = sem("s_wlo")
        s_T = sem("s_T")
        s_xhi = sem("s_xhi")
        s_xlo = sem("s_xlo")
        s_h1 = sem("s_h1")
        s_h3 = sem("s_h3")
        s_sil = sem("s_sil")
        s_hid = sem("s_hid")
        s_y = sem("s_y")
        s_yc = sem("s_yc")
        s_got = [sem(f"s_got_{b}") for b in range(SLOT3)]
        s_comb = sem("s_comb")
        s_ch2 = sem("s_ch2")
        s_store = sem("s_store")

        x_q = x.rearrange("b l d -> (b l) d").rearrange("(q j p) d -> q p j d", q=QUARTERS, p=P)
        out_t = out.rearrange("b l d -> (b l) d").rearrange("(j p) d -> p j d", p=P)
        xs_fill = xs_dram.rearrange("(f p r) d -> f p r d", f=FILLS, p=P)
        xs_tile = xs_dram.rearrange("(t j p) d -> p t j d", p=P, j=GT)
        ys_tile = ys_dram.rearrange("(t j p) d -> p t j d", p=P, j=GT)

        ctx.enter_context(nc.allow_non_contiguous_dma(reason="three vectors of 256 elements"))
        block = ctx.enter_context(nc.Block())

        def phase(step, first, last):
            step(first - 1, 2, True, False, False)
            step(first, 0, True, True, False)
            return first + 1, (last - first - 2) // SLOT3

        def mixer(eng, step, first, last):
            g0, turns = phase(step, first, last)
            with eng.Fori(0, turns) as i:
                for k in range(SLOT3):
                    step(i * SLOT3 + (g0 + k), (k + 1) % SLOT3, True, True, True)
            n = last - first
            step(last - 1, (n - 1) % SLOT3, False, True, True)
            step(last, n % SLOT3, False, False, True)

        @block.sync
        def _(sp):
            sp.dma_start(win_raw, W_in.rearrange("(a p) h -> p a h", p=P)).then_inc(s_wld, 16)
            sp.dma_start(wdt_raw, W_dt.rearrange("(a p) k -> p a k", p=P)).then_inc(s_wld, 16)
            sp.dma_start(wx_raw, W_x[2 * STATE:, :].rearrange("(a p) i -> p a i", p=P)).then_inc(s_wld, 16)
            sp.dma_start(wxB, W_x[0:STATE, :]).then_inc(s_wld, 16)
            sp.dma_start(wxC, W_x[STATE:2 * STATE, :]).then_inc(s_wld, 16)
            sp.dma_start(wo_raw, W_out).then_inc(s_wld, 16)
            sp.dma_start(wg[:, :], w_gate).then_inc(s_wld, 16)
            sp.dma_start(cw[:, :, :], conv_w.rearrange("(c p) o k -> p c (o k)", p=P)).then_inc(s_wld, 16)
            sp.dma_start(cb[:, :], conv_b.rearrange("(c p) -> p c", p=P)).then_inc(s_wld, 16)
            sp.dma_start(bdt[:, :], b_dt.rearrange("(c p) -> p c", p=P)).then_inc(s_wld, 16)
            sp.dma_start(dsk[:, :], D_skip.rearrange("(c p) -> p c", p=P)).then_inc(s_wld, 16)
            sp.wait_ge(s_zrow, 1)
            for f in range(FILLS):
                sp.dma_start(xs_fill[f], zrow[:, :, :].broadcast_to([P, FILL_ROWS, D])).then_inc(s_fill, 16)

            def load(t, n, b, first):
                e = sp.value_load(eid_i[0:1, bass.ds(t, 1)] if not isinstance(t, int) else eid_i[0:1, t:t + 1],
                                  min_val=0, max_val=EXPERTS - 1)
                if not first:
                    sp.wait_ge(s_whi, t - 1)
                    sp.wait_ge(s_wlo, t - 1)
                dst = w13[b].rearrange("p (a h) -> p a h", a=2)
                sp.dma_start(dst[:, 0, :], w1[bass.ds(e, 1)].rearrange("e d h -> d (e h)")).then_inc(s_w13[b], 16)
                sp.dma_start(dst[:, 1, :], w3[bass.ds(e, 1)].rearrange("e d h -> d (e h)")).then_inc(s_w13[b], 16)
                if not first:
                    sp.wait_ge(s_T, t - 1)
                src = xs_tile[:, t:t + 1] if isinstance(t, int) else xs_tile[:, bass.ds(t, 1)]
                sp.dma_start(xs[b].rearrange("p (o j d) -> p o j d", o=1, j=GT), src).then_inc(s_xs[b], 16)
                if not first:
                    sp.wait_ge(s_y, t - 1)
                sp.dma_start(w2b[b].rearrange("p (o k d) -> p o k d", o=1, k=HALVES),
                             w2[bass.ds(e, 1)].rearrange("e (k p) d -> p e k d", p=P)).then_inc(s_w2[b], 16)

            def store(t, b):
                sp.wait_ge(s_yc, t + 1)
                dst = ys_tile[:, t:t + 1] if isinstance(t, int) else ys_tile[:, bass.ds(t, 1)]
                sp.dma_start(dst, yo[b].rearrange("p (o j d) -> p o j d", o=1, j=GT)).then_inc(s_ys[b], 16)

            sp.wait_ge(s_eid, 1)
            sp.wait_ge(s_scat, 16 * TOP_K * TILES)
            load(0, 0, 0, True)
            load(1, 0, 1, True)
            with sp.Fori(0, (MOE_TILES - 3) // 2) as i:
                load(i * 2 + 2, i + 1, 0, False)
                store(i * 2, 0)
                load(i * 2 + 3, i + 1, 1, False)
                store(i * 2 + 1, 1)
            load(MOE_TILES - 1, 0, 0, False)
            for t in range(MOE_TILES - 3, MOE_TILES):
                store(t, t % 2)

            for k in range(GROUPS // 2):
                sp.wait_ge(s_add, 2 * k + 2)
                sp.wait_ge(s_comb, k + 1)
                at = slice(2 * k * GT, (2 * k + 2) * GT)
                sp.dma_start(out_t[:, at], xacc[:, at]).then_inc(s_store, 16)
            sp.wait_ge(s_store, 16 * (GROUPS // 2))

        @block.gpsimd
        def _(gp):
            gp.memset(ident[:, :], 0.0).then_inc(s_cst, 1)
            gp.memset(tri, 0.0).then_inc(s_cst, 1)
            gp.memset(ones_pp, 1.0).then_inc(s_cst, 1)
            gp.memset(inv16, 1.0 / STATE).then_inc(s_cst, 1)
            gp.memset(ones64, 1.0).then_inc(s_cst, 1)
            gp.iota(iot[:, 0:128], [[0, EXPERTS], [SLOTS, 16]], base=0, channel_multiplier=0).then_inc(s_cst, 1)
            gp.iota(iot[:, 128:128 + EXPERTS], [[-1, EXPERTS]], base=EXPERTS, channel_multiplier=0).then_inc(s_cst, 1)
            gp.iota(iot[:, 256:256 + MOE_TILES], [[1, MOE_TILES]], base=0, channel_multiplier=0).then_inc(s_cst, 1)
            gp.wait_ge(s_cst, 8)
            gp.affine_select(out=ident[:, :], in_=ident[:, :], compare_op=ALU.not_equal, fill=1.0,
                             base=0, pattern=[[-1, P]], channel_multiplier=1).then_inc(s_cst, 1)
            gp.affine_select(out=tri, in_=tri, compare_op=ALU.is_ge, fill=1.0,
                             base=0, pattern=[[-1, P]], channel_multiplier=1).then_inc(s_cst, 1)
            for q in range(QUARTERS):
                if q:
                    gp.wait_ge(s_x, 16 * q)
                gp.dma_start(xacc[:, q * QT:(q + 1) * QT, :], x_q[q]).then_inc(s_x, 16)
            gp.wait_ge(s_fill, 16 * FILLS)
            gp.wait_ge(s_slot, 1)
            for j in range(TILES):
                for k in range(TOP_K):
                    gp.indirect_dma_start(xs_dram, bass.IndirectOffsetOnAxis(ap=slot_u[:, k, j:j + 1], axis=0),
                                          xn[:, j * D:(j + 1) * D], None).then_inc(s_scat, 16)

            def step(t, n, b, more):
                gp.wait_ge(s_whi, t + 1)
                if not (isinstance(t, int) and t < 2):
                    gp.wait_ge(s_h3, t - 1)
                gp.tensor_tensor(wlo[:, b, :], w13[b], whi[:, b, :].bitcast(F32), ALU.subtract).then_inc(s_wlo, 1)
            step(0, 0, 0, True)
            step(1, 0, 1, True)
            with gp.Fori(0, (MOE_TILES - 3) // 2) as i:
                step(i * 2 + 2, i + 1, 0, True)
                step(i * 2 + 3, i + 1, 1, True)
            step(MOE_TILES - 1, 0, 0, False)

            gp.wait_ge(s_ys[0], 16 * ((MOE_TILES + 1) // 2))
            gp.wait_ge(s_ys[1], 16 * (MOE_TILES // 2))
            for k in range(GROUPS // 2):
                if k >= SLOT3:
                    gp.wait_ge(s_comb, k - SLOT3 + 1)
                for g in range(2):
                    for c in range(TOP_K):
                        for j in range(GT):
                            tile = (2 * k + g) * GT + j
                            gp.indirect_dma_start(
                                got[k % SLOT3][:, g, c, j, :], None, ys_dram,
                                bass.IndirectOffsetOnAxis(ap=slot_u[:, c, tile:tile + 1], axis=0),
                            ).then_inc(s_got[k % SLOT3], 16)

        @block.tensor
        def _(pe):
            pe.wait_ge(s_wld, 16 * 11)
            pe.wait_ge(s_cst, 10)
            for a in range(4):
                pe.transpose(PA[:, a * P:(a + 1) * P], win_raw[:, a, :], ident[:, :]).then_inc(s_wtp, 1)
            for kb in range(2):
                for ob in range(2):
                    at = 512 + kb * 256 + ob * 128
                    pe.transpose(PA[:, at:at + P], wdt_raw[:, ob, kb * P:(kb + 1) * P], ident[:, :]).then_inc(s_wtp, 1)
            for ib in range(2):
                pe.transpose(PB[:, 512 + ib * P:512 + (ib + 1) * P], wo_raw[:, ib * P:(ib + 1) * P],
                             ident[:, :]).then_inc(s_wtp, 1)
            for n, rows in enumerate((wxB, wxC)):
                for ib in range(2):
                    at = (n * 2 + ib) * P
                    pe.matmul(PC[:, at:at + P], rows[:, ib * P:(ib + 1) * P], inv16, start=True, stop=True).then_inc(s_wtp, 1)
            pe.wait_ge(s_wcp, 2)
            for ib in range(2):
                for kb in range(2):
                    pe.matmul(PB[:, ib * 256:(ib + 1) * 256], wx_raw[:, kb, ib * P:(ib + 1) * P], wdtT[:, kb, :],
                              start=(kb == 0), stop=(kb == 1)).then_inc(s_wtp, 1)
            def logits(g):
                pe.wait_ge(s_xnT, g + 1)
                for j in range(GT * g, GT * g + GT):
                    last = pe.matmul(PC[:, 512 + j * EXPERTS:512 + (j + 1) * EXPERTS], xnT[:, j * P:(j + 1) * P],
                                     wg[:, :], start=True, stop=True)
                last.then_inc(s_lg, 1)

            pe.wait_ge(s_wcp, 5)
            for g in range(GROUPS):
                pe.wait_ge(s_xn, g + 1)
                if g >= 2:
                    pe.wait_ge(s_xnT, g - 1)
                for j in range(GT):
                    t = g * GT + j
                    at = (g % 2) * 512 + j * P
                    last = pe.transpose(PA[:, at:at + P], xn[:, t * D:(t + 1) * D], ident[:, :])
                last.then_inc(s_xt, 1)
                if g:
                    logits(g - 1)
            logits(GROUPS - 1)
            pe.wait_ge(s_msk, 1)
            pe.matmul(PD[:, 0:512], tri, msk.rearrange("p j e -> p (j e)"), start=True, stop=True).then_inc(s_rk, 1)
            pe.matmul(PD[:, 512:1024], ones_pp, msk.rearrange("p j e -> p (j e)"), start=True, stop=True).then_inc(s_rk, 1)

            def mix(g, slot, a, b, c):
                static = isinstance(g, int)
                nxt = (slot + 1) % SLOT3
                if b:
                    pe.wait_ge(s_xc, g + 1)
                    if not (static and g < 1):
                        pe.wait_ge(s_dt, g)
                    else:
                        pe.wait_ge(s_slot, 1)
                    for c_ in range(HALVES):
                        for k in range(HALVES):
                            last = pe.matmul(PC[:, c_ * GROUP:(c_ + 1) * GROUP], Wc[:, k, c_ * P:(c_ + 1) * P],
                                             xc[:, slot, k, :], start=(k == 0), stop=(k == 1))
                    last.then_inc(s_u, 1)
                if a:
                    if not (static and g + 1 < 1):
                        pe.wait_ge(s_taps, g + 1)
                        pe.wait_ge(s_sz, g + 1)
                    src = xnT[:, bass.ds(g * GROUP + GROUP, GROUP)] if not static else \
                        xnT[:, (g + 1) * GROUP:(g + 2) * GROUP]
                    for c_ in range(HALVES):
                        last = pe.matmul(PA[:, c_ * GROUP:(c_ + 1) * GROUP], WinT[:, c_ * P:(c_ + 1) * P], src,
                                         start=True, stop=True)
                    last.then_inc(s_xp, 1)
                    for c_ in range(HALVES):
                        last = pe.matmul(PB[:, c_ * GROUP:(c_ + 1) * GROUP],
                                         WinT[:, INNER + c_ * P:INNER + (c_ + 1) * P], src, start=True, stop=True)
                    last.then_inc(s_z, 1)
                if c:
                    pe.wait_ge(s_y2, g)
                    pe.wait_ge(s_thg, g)
                    for j in range(GT):
                        for k in range(HALVES):
                            last = pe.matmul(PD[:, j * D:(j + 1) * D], y2[:, k, j * P:(j + 1) * P], WoT[:, k, :],
                                             start=(k == 0), stop=(k == 1))
                    last.then_inc(s_out, 1)
                if b:
                    if c:
                        pe.wait_ge(s_add, g)
                    for n in range(2):
                        for k in range(HALVES):
                            last = pe.matmul(PD[:, n * GROUP:(n + 1) * GROUP], WgB[:, n * 2 + k, :],
                                             xc[:, slot, k, :], start=(k == 0), stop=(k == 1))
                    last.then_inc(s_g, 1)

            pe.wait_ge(s_xnT, GROUPS)
            pe.wait_ge(s_slot, 1)
            mixer(pe, mix, 0, HALF_GROUPS)

            def transp(t, n, b, first):
                pe.wait_ge(s_xs[b], n * 16 + 16)
                if not first:
                    pe.wait_ge(s_xhi, t)
                    pe.wait_ge(s_xlo, t)
                for j in range(GT):
                    last = pe.transpose(PC[:, j * P:(j + 1) * P], xs[b][:, j * D:(j + 1) * D], ident[:, :])
                last.then_inc(s_T, 1)

            def up(t, b, first):
                pe.wait_ge(s_wlo, t + 1)
                pe.wait_ge(s_xlo, t + 1)
                pe.wait_ge(s_xhi, t + 1)
                for m, (ps, free, done) in enumerate(((PA, s_sil, s_h1), (PB, s_hid, s_h3))):
                    if not first:
                        pe.wait_ge(free, t)
                    for c_ in range(HALVES):
                        at = m * HID + c_ * P
                        o = ps[:, c_ * SLOTS:(c_ + 1) * SLOTS]
                        pe.matmul(o, whi[:, b, at:at + P], xhi[:, b, :], start=True, stop=False)
                        pe.matmul(o, whi[:, b, at:at + P], xlo[:, b, :], start=False, stop=False)
                        last = pe.matmul(o, wlo[:, b, at:at + P], xhi[:, b, :], start=False, stop=True)
                    last.then_inc(done, 1)

            def down(t, n, b, first):
                pe.wait_ge(s_hid, t + 1)
                pe.wait_ge(s_w2[b], n * 16 + 16)
                if not first:
                    pe.wait_ge(s_yc, t)
                for j in range(GT):
                    for k in range(HALVES):
                        last = pe.matmul(PC[:, 512 + j * D:512 + (j + 1) * D],
                                         hid[b][:, k * SLOTS + j * P:k * SLOTS + (j + 1) * P],
                                         w2b[b][:, k * D:(k + 1) * D], start=(k == 0), stop=(k == 1))
                last.then_inc(s_y, 1)

            pe.wait_ge(s_dt, HALF_GROUPS)
            pe.wait_ge(s_taps, HALF_GROUPS)
            pe.wait_ge(s_sz, HALF_GROUPS)
            transp(0, 0, 0, True)
            up(0, 0, True)
            transp(1, 0, 1, False)
            up(1, 1, False)
            down(0, 0, 0, True)
            transp(2, 1, 0, False)
            with pe.Fori(0, (MOE_TILES - 3) // 2) as i:
                up(i * 2 + 2, 0, False)
                down(i * 2 + 1, i, 1, False)
                transp(i * 2 + 3, i + 1, 1, False)
                up(i * 2 + 3, 1, False)
                down(i * 2 + 2, i + 1, 0, False)
                transp(i * 2 + 4, i + 2, 0, False)
            t = MOE_TILES - 1
            up(t, 0, False)
            down(t - 1, (t - 1) // 2, 1, False)
            down(t, t // 2, 0, False)

            pe.wait_ge(s_sil, MOE_TILES)
            pe.wait_ge(s_hid, MOE_TILES)
            pe.wait_ge(s_yc, MOE_TILES)
            mixer(pe, mix, HALF_GROUPS, GROUPS)

        @block.scalar
        def _(act):
            act.preload_act_table_set("sqrt_and_others")
            act.wait_ge(s_wtp, 4)
            act.activation(WinT[:, :], PA[:, 0:512], ACT.Copy).then_inc(s_wcp, 1)
            act.wait_ge(s_wtp, 8)
            act.activation(wdtT, PA[:, 512:1024].rearrange("p (a b) -> p a b", a=2), ACT.Copy).then_inc(s_wcp, 1)
            act.wait_ge(s_wtp, 10)
            act.activation(WoT[:, :, :], PB[:, 512:768].rearrange("p (a b) -> p a b", a=2), ACT.Copy,
                           scale=-0.125).then_inc(s_wcp, 1)
            act.wait_ge(s_wtp, 14)
            act.activation(WgB[:, :, :], PC[:, 0:512].rearrange("p (a b) -> p a b", a=4), ACT.Copy).then_inc(s_wcp, 1)
            act.wait_ge(s_wtp, 18)
            act.activation(Wc[:, :, :], PB[:, 0:512].rearrange("p (a b) -> p a b", a=2), ACT.Copy).then_inc(s_wcp, 1)
            act.activation(dsk8[:, :], dsk[:, :], ACT.Copy, scale=-8.0).then_inc(s_wcp, 1)
            for q in range(QUARTERS):
                act.wait_ge(s_var, q + 1)
                act.activation(std, var, ACT.Sqrt).then_inc(s_std, 1)
                for g in range(q * GROUPS // QUARTERS, (q + 1) * GROUPS // QUARTERS):
                    act.wait_ge(s_xt, g + 1)
                    act.activation(xnT[:, g * GROUP:(g + 1) * GROUP], PA[:, (g % 2) * 512:(g % 2) * 512 + 512],
                                   ACT.Copy).then_inc(s_xnT, 1)
            act.wait_ge(s_dlt, 1)
            act.activation(den, dlt, ACT.Exp).then_inc(s_edl, 1)

            def mix(g, slot, a, b, c):
                static = isinstance(g, int)
                nxt = (slot + 1) % SLOT3
                if b:
                    act.preload_act_table_set("natural_log_exp_and_others")
                    act.wait_ge(s_cap, g + 1)
                    act.activation(ebuf[:, :, :], ebuf[:, :, :], ACT.Exp).then_inc(s_exp, 1)
                    act.wait_ge(s_exp, g + 1)
                    act.activation(ebuf[:, :, :], ebuf[:, :, :], ACT.Ln, bias=1.0).then_inc(s_ln, 1)
                if a:
                    act.wait_ge(s_xp, g + 2)
                    if not (static and g + 1 < 1):
                        act.wait_ge(s_xc, g + 1)
                    for c_ in range(HALVES):
                        last = act.activation(acc[:, c_, :], PA[:, c_ * GROUP:(c_ + 1) * GROUP], ACT.Identity,
                                              bias=cb[:, c_:c_ + 1], scale=cw[:, c_, TAPS - 1:TAPS])
                    last.then_inc(s_tap0, 1)
                act.preload_act_table_set("silu_and_others")
                if b:
                    act.wait_ge(s_dt, g + 1)
                    if c:
                        act.wait_ge(s_ch, g * CHAIN - CHAIN + 2)
                    act.activation(th[:, :, :], ebuf[:, :, :], ACT.Tanh, scale=0.05).then_inc(s_th, 1)
                    act.wait_ge(s_th, g + 1)
                    if c:
                        act.wait_ge(s_ch, g * CHAIN - CHAIN + 5)
                    act.activation(al[:, :, :], th[:, :, :], ACT.Copy, bias=0.5, scale=0.5).then_inc(s_al, 1)
                if a:
                    act.wait_ge(s_z, g + 2)
                    act.activation(sz[:, nxt].rearrange("p a b -> p (a b)"), PB[:, :], ACT.Silu).then_inc(s_sz, 1)
                    act.wait_ge(s_taps, g + 2)
                    act.activation(xc[:, nxt], acc[:, :, :], ACT.Silu).then_inc(s_xc, 1)
                if b:
                    act.wait_ge(s_g, g + 1)
                    if c:
                        act.wait_ge(s_ch, g * CHAIN - CHAIN + 6)
                    act.activation(thg[:, :, :].rearrange("p a b -> p (a b)"), PD[:, :], ACT.Tanh,
                                   scale=0.5).then_inc(s_thg, 1)

            act.wait_ge(s_slot, 1)
            act.wait_ge(s_eid, 1)
            mixer(act, mix, 0, HALF_GROUPS)

            def split_x(t, n, b, first):
                act.wait_ge(s_w13[b], n * 32 + 32)
                if not first:
                    act.wait_ge(s_h3, t - 1)
                act.activation(whi[:, b, :], w13[b], ACT.Copy).then_inc(s_whi, 1)
                act.wait_ge(s_T, t + 1)
                act.activation(xhi[:, b, :], PC[:, 0:512], ACT.Copy).then_inc(s_xhi, 1)

            def gate(t, first):
                act.wait_ge(s_h1, t + 1)
                if not first:
                    act.wait_ge(s_hid, t)
                act.activation(sil, PA[:, :], ACT.Silu).then_inc(s_sil, 1)

            def copy_y(t, n, b, first):
                act.wait_ge(s_y, t + 1)
                if not first:
                    act.wait_ge(s_ys[b], n * 16)
                act.activation(yo[b], PC[:, 512:1024], ACT.Copy).then_inc(s_yc, 1)

            split_x(0, 0, 0, True)
            split_x(1, 0, 1, True)
            gate(0, True)
            gate(1, False)
            copy_y(0, 0, 0, True)
            split_x(2, 1, 0, False)
            gate(2, False)
            copy_y(1, 0, 1, True)
            split_x(3, 1, 1, False)
            with act.Fori(0, (MOE_TILES - 5) // 2) as i:
                gate(i * 2 + 3, False)
                copy_y(i * 2 + 2, i + 1, 0, False)
                split_x(i * 2 + 4, i + 2, 0, False)
                gate(i * 2 + 4, False)
                copy_y(i * 2 + 3, i + 1, 1, False)
                split_x(i * 2 + 5, i + 2, 1, False)
            t = MOE_TILES - 2
            gate(t, False)
            copy_y(t - 1, (t - 1) // 2, 0, False)
            split_x(t + 1, (t + 1) // 2, 0, False)
            gate(t + 1, False)
            copy_y(t, t // 2, 1, False)
            copy_y(t + 1, (t + 1) // 2, 0, False)

            mixer(act, mix, HALF_GROUPS, GROUPS)

        @block.vector
        def _(ve):
            count = [0]

            def link(ins):
                count[0] += 1
                ins.then_inc(s_dve, 1)
                ve.wait_ge(s_dve, count[0])

            ve.memset(zrow[:, :, :], 0.0).then_inc(s_zrow, 1)
            for q in range(QUARTERS):
                ve.wait_ge(s_x, 16 * (q + 1))
                for j in range(QT):
                    last = ve.bn_stats(st[:, j, :], xacc[:, q * QT + j, :])
                link(last)
                for j in range(QT):
                    last = ve.bn_aggr(mv[:, j, :], st[:, j, :])
                link(last)
                ve.tensor_scalar(var, mv[:, :, 1], EPS, None, ALU.add).then_inc(s_var, 1)
                ve.wait_ge(s_var, q + 1)
                ve.wait_ge(s_std, q + 1)
                link(ve.reciprocal(rst, std))
                link(ve.tensor_tensor(nrt, rst, rst, ALU.mult))
                link(ve.tensor_tensor(nrt, nrt, var, ALU.mult))
                link(ve.tensor_scalar(nrt, nrt, -0.5, 1.5, ALU.mult, ALU.add))
                link(ve.tensor_tensor(rst, rst, nrt, ALU.mult))
                for j in range(QT):
                    t = q * QT + j
                    last = ve.tensor_scalar(xn[:, t * D:(t + 1) * D], xacc[:, t, :], mv[:, j, 0:1], rst[:, j:j + 1],
                                            ALU.subtract, ALU.mult)
                    if j % GT == GT - 1:
                        last.then_inc(s_xn, 1)
                ve.wait_ge(s_xn, (q + 1) * QT // GT)
            ve.wait_ge(s_cst, 10)
            ve.tensor_copy(thr, iot[:, 0:128].rearrange("p (e m) -> p e m", e=EXPERTS))
            ve.tensor_copy(rev, iot[:, 128:128 + EXPERTS])
            link(ve.tensor_copy(tix, iot[:, 256:256 + MOE_TILES]))
            ve.wait_ge(s_lg, GROUPS)
            link(ve.tensor_copy(L, je(PC[:, 512:1024])))

            def bc(v):
                return v.unsqueeze(2).broadcast_to([P, TILES, EXPERTS])
            rev_b = rev.unsqueeze(1).broadcast_to([P, TILES, EXPERTS])

            def pick(logit, best, oh):
                link(ve.reduce_max(best, logit, AX_X))
                link(ve.tensor_tensor(tmp, logit, bc(best), ALU.is_equal))
                link(ve.tensor_tensor(tmp, tmp, rev_b, ALU.mult))
                link(ve.reduce_max(c1, tmp, AX_X))
                link(ve.tensor_tensor(oh, rev_b, bc(c1), ALU.is_equal))
            pick(L, m1, oh1)
            link(ve.scalar_tensor_tensor(L2, oh1, -3.0e38, L, ALU.mult, ALU.add))
            pick(L2, m2, oh2)
            ve.tensor_tensor(msk, oh1, oh2, ALU.add).then_inc(s_msk, 1)
            ve.tensor_tensor(dlt, m2, m1, ALU.subtract).then_inc(s_dlt, 1)
            ve.wait_ge(s_edl, 1)
            link(ve.tensor_scalar(c1, den, 1.0, None, ALU.add))
            link(ve.reciprocal(prob[:, 0, :], c1))
            link(ve.tensor_tensor(prob[:, 1, :], prob[:, 0, :], den, ALU.mult))
            ve.wait_ge(s_rk, 2)
            link(ve.tensor_copy(tot, je(PD[:, 512:1024])))
            for e in range(EXPERTS):
                last = ve.tensor_tensor_scan(inc[:, :, e], ones64, tot[:, :, e], 0.0, ALU.mult, ALU.add)
            link(last)
            cnt_b = inc[:, TILES - 1, :].unsqueeze(2).broadcast_to([P, EXPERTS, 16])
            link(ve.tensor_tensor(cmp_m, thr, cnt_b, ALU.is_lt))
            link(ve.reduce_sum(nte, cmp_m, AX_X))
            link(ve.tensor_tensor_scan(nti, ones64[:, 0:EXPERTS], nte, 0.0, ALU.mult, ALU.add))
            link(ve.tensor_tensor(base, nti, nte, ALU.subtract))
            link(ve.tensor_tensor(tmp, inc, tot, ALU.subtract))
            link(ve.tensor_tensor(tmp, tmp, je(PD[:, 0:512]), ALU.add))
            base_b = base.unsqueeze(1).broadcast_to([P, TILES, EXPERTS])
            link(ve.scalar_tensor_tensor(tmp, base_b, float(SLOTS), tmp, ALU.mult, ALU.add))
            for k, oh in enumerate((oh1, oh2)):
                link(ve.tensor_tensor(L2, oh, tmp, ALU.mult))
                link(ve.reduce_sum(sf[:, k, :], L2, AX_X))
            ve.tensor_copy(slot_u[:, :, :], sf).then_inc(s_slot, 1)
            link(ve.tensor_tensor(cmp_t, nti.unsqueeze(1).broadcast_to([P, MOE_TILES, EXPERTS]),
                                  tix.unsqueeze(2).broadcast_to([P, MOE_TILES, EXPERTS]), ALU.is_le))
            link(ve.reduce_sum(eid_f, cmp_t, AX_X))
            link(ve.tensor_scalar(eid_f, eid_f, float(EXPERTS - 1), None, ALU.min))
            ve.tensor_copy(eid_i[:, :], eid_f).then_inc(s_eid, 1)
            ve.wait_ge(s_slot, 1)
            ve.wait_ge(s_eid, 1)

            def mix(g, slot, a, b, c):
                static = isinstance(g, int)
                nxt, prv = (slot + 1) % SLOT3, (slot + 2) % SLOT3
                now = [0]

                def step(ins):
                    now[0] += 1
                    ins.then_inc(s_ch, 1)

                def after(n):
                    ve.wait_ge(s_ch, g * CHAIN - CHAIN + n)
                if c:
                    ve.wait_ge(s_al, g)
                    step(ve.tensor_scalar(al[:, :, :], al[:, :, :], 0.01, 0.99, ALU.max, ALU.min))
                    step(ve.scalar_tensor_tensor(gbuf[:, :, :], th[:, :, :], -1.0, xc[:, prv], ALU.add, ALU.mult))
                    after(1)
                    step(ve.memset(al[:, :, :].rearrange("p a (s l) -> p a s l", s=SPG)[:, :, :, 0], 0.0))
                    ve.wait_ge(s_thg, g)
                    after(2)
                    step(ve.scalar_tensor_tensor(gbuf[:, :, :], thg[:, 0:1, :].broadcast_to([P, HALVES, GROUP]), 1.0,
                                                 gbuf[:, :, :], ALU.add, ALU.mult))
                    after(4)
                    step(ve.tensor_tensor_scan(hbuf[:, :, :].rearrange("p a b -> p (a b)"),
                                               al[:, :, :].rearrange("p a b -> p (a b)"),
                                               gbuf[:, :, :].rearrange("p a b -> p (a b)"), 0.0, ALU.mult, ALU.add))
                    after(5)
                    step(ve.scalar_tensor_tensor(ybuf[:, :, :], thg[:, 1:2, :].broadcast_to([P, HALVES, GROUP]), 1.0,
                                                 hbuf[:, :, :], ALU.add, ALU.mult))
                if b:
                    ve.wait_ge(s_u, g + 1)
                    if not (static and g < 1):
                        ve.wait_ge(s_th, g)
                    for c_ in range(HALVES):
                        last = ve.tensor_scalar(ebuf[:, c_, :], PC[:, c_ * GROUP:(c_ + 1) * GROUP],
                                                bdt[:, c_:c_ + 1], EXP_CAP, ALU.add, ALU.min)
                    last.then_inc(s_cap, 1)
                if c:
                    after(6)
                    for c_ in range(HALVES):
                        last = ve.scalar_tensor_tensor(ybuf[:, c_, :], xc[:, prv, c_, :], dsk8[:, c_:c_ + 1],
                                                       ybuf[:, c_, :], ALU.mult, ALU.add)
                    step(last)
                    after(7)
                    if not (static and g < 2):
                        ve.wait_ge(s_out, g - 1)
                    step(ve.tensor_tensor(y2[:, :, :], ybuf[:, :, :], sz[:, prv], ALU.mult))
                    after(8)
                    ve.sem_inc(s_y2, 1)
                if b:
                    ve.wait_ge(s_ln, g + 1)
                    for c_ in range(HALVES):
                        last = ve.scalar_tensor_tensor(ebuf[:, c_, :], PC[:, c_ * GROUP:(c_ + 1) * GROUP],
                                                       bdt[:, c_:c_ + 1], ebuf[:, c_, :], ALU.add, ALU.max)
                    last.then_inc(s_dt, 1)

                def taps(j):
                    if j > 1:
                        ve.wait_ge(s_cv, g * 2 + j + 1)
                    for c_ in range(HALVES):
                        a_v = acc[:, c_, :].rearrange("p (s l) -> p s l", s=SPG)[:, :, j:SEQ]
                        last = ve.scalar_tensor_tensor(
                            a_v, PA[:, c_ * GROUP:(c_ + 1) * GROUP].rearrange("p (s l) -> p s l", s=SPG)[:, :, 0:SEQ - j],
                            cw[:, c_, TAPS - 1 - j:TAPS - j], a_v, ALU.mult, ALU.add)
                    last.then_inc(s_taps if j == TAPS - 1 else s_cv, 1)
                if a:
                    ve.wait_ge(s_tap0, g + 2)
                    taps(1)
                    taps(2)
                if c:
                    ve.wait_ge(s_out, g)
                    at = bass.ds(g * GT - GT, GT) if not static else slice((g - 1) * GT, g * GT)
                    ve.tensor_tensor(xacc[:, at, :], PD[:, 0:GROUP].rearrange("p (j d) -> p j d", j=GT),
                                     xacc[:, at, :], ALU.add).then_inc(s_add, 1)
                if a:
                    taps(3)

            mixer(ve, mix, 0, HALF_GROUPS)

            def low(t, b, first):
                ve.wait_ge(s_xhi, t + 1)
                if not first:
                    ve.wait_ge(s_h3, t - 1)
                ve.tensor_tensor(xlo[:, b, :], PC[:, 0:512], xhi[:, b, :].bitcast(F32), ALU.subtract).then_inc(s_xlo, 1)

            def glu(t, b, first):
                ve.wait_ge(s_h3, t + 1)
                ve.wait_ge(s_sil, t + 1)
                if not first:
                    ve.wait_ge(s_y, t - 1)
                ve.tensor_tensor(hid[b], sil, PB[:, :], ALU.mult).then_inc(s_hid, 1)

            low(0, 0, True)
            low(1, 1, True)
            glu(0, 0, True)
            low(2, 0, False)
            glu(1, 1, True)
            with ve.Fori(0, (MOE_TILES - 3) // 2) as i:
                low(i * 2 + 3, 1, False)
                glu(i * 2 + 2, 0, False)
                low(i * 2 + 4, 0, False)
                glu(i * 2 + 3, 1, False)
            glu(MOE_TILES - 1, 0, False)

            def add_pair(k, slot, filled, added=0):
                ve.wait_ge(s_got[slot], filled)
                ve.wait_ge(s_add, added or k + HALF_GROUPS)
                for ch in range(TOP_K):
                    if ch:
                        ve.wait_ge(s_ch2, k + 1)
                    for n in range(2):
                        for j in range(GT):
                            tile = k * (2 * GT) + (n * GT + j)
                            at = slice(tile, tile + 1) if isinstance(tile, int) else bass.ds(tile, 1)
                            dst = xacc[:, at, :].rearrange("p o d -> p (o d)")
                            last = ve.scalar_tensor_tensor(dst, got[slot][:, n, ch, j, :], prob[:, ch, at],
                                                           dst, ALU.mult, ALU.add)
                    last.then_inc(s_comb if ch else s_ch2, 1)

            filled = 16 * 2 * TOP_K * GT
            g0, turns = phase(mix, HALF_GROUPS, GROUPS)
            add_pair(0, 0, filled)
            with ve.Fori(0, turns) as i:
                for m in range(SLOT3):
                    slot = (m + 1) % SLOT3
                    mix(i * SLOT3 + (g0 + m), slot, True, True, True)
                    add_pair(i * SLOT3 + (m + 1), slot, i * filled + (2 * filled if slot == 0 else filled))
            n = HALF_GROUPS
            mix(GROUPS - 1, (n - 1) % SLOT3, False, True, True)
            mix(GROUPS, n % SLOT3, False, False, True)
            add_pair(n - 1, (n - 1) % SLOT3, filled * ((n - 1) // SLOT3 + 1), GROUPS)


_INS = ['L0_attn_x', 'L0_attn_W_in', 'L0_attn_conv_w', 'L0_attn_conv_b', 'L0_attn_W_x', 'L0_attn_W_dt',
        'L0_attn_b_dt', 'L0_attn_A_log', 'L0_attn_D', 'L0_attn_W_out', 'L0_ffn_w_gate', 'L0_ffn_w1',
        'L0_ffn_w3', 'L0_ffn_w2']
_OUTS = [((BATCH, SEQ, D), 'float32')]


def kernel(**inputs):
    import numpy as _np
    import concourse.bacc as _bacc
    from concourse import mybir as _mybir
    from concourse.bass_utils import run_bass_kernel_spmd as _run

    nc = _bacc.Bacc("TRN2", target_bir_lowering=False, num_devices=1)
    arrays, args = {}, []
    for name in _INS:
        a = _np.ascontiguousarray(inputs[name])
        arrays[f"in_{name}_dram"] = a
        args.append(nc.dram_tensor(f"in_{name}_dram", a.shape, _mybir.dt.from_np(a.dtype), kind="ExternalInput").ap())
    for i, (shape, dtype) in enumerate(_OUTS):
        dt = _mybir.dt.from_np(_np.dtype(dtype))
        args.append(nc.dram_tensor(f"out_{i}_dram", shape, dt, kind="ExternalOutput").ap())
    block_kernel(nc, *args)
    r = _run(nc, [arrays], core_ids=[0])
    return r.results[0]["out_0_dram"]
```

```python
import concourse.bass as bass
from concourse import mybir
from contextlib import ExitStack

F32 = mybir.dt.float32
F32R = mybir.dt.float32r
I32 = mybir.dt.int32
U32 = mybir.dt.uint32
ALU = mybir.AluOpType
ACT = mybir.ActivationFunctionType
AX_X = mybir.AxisListType.X

P = 128
BATCH, SEQ, D = 32, 256, 128
TOKENS = BATCH * SEQ
TILES = TOKENS // P
GROUP = 512
GROUPS = TOKENS // GROUP
GT = GROUP // P
SPG = GROUP // SEQ
INNER, STATE, TAPS = 256, 16, 4
HALVES = INNER // P
EXPERTS, HID, TOP_K = 8, 256, 2
SLOTS = 512
PAIRS = TOKENS * TOP_K
MOE_TILES = (PAIRS + EXPERTS * (SLOTS - 1)) // SLOTS
EPS = 1e-5
QUARTERS = 4
QT = TILES // QUARTERS
STEPS_A = 8
EXP_CAP = 40.0
SLOT3 = 3
REGION = TOKENS + SLOTS
CHUNKS = ((0, 1), (1, 3))
SETUP_AT = (5, 7, 9)
FIRST_PAIR = 9
CHAIN = 7


def block_kernel(nc, x, W_in, conv_w, conv_b, W_x, W_dt, b_dt, A_log, D_skip, W_out,
                 w_gate, w1, w3, w2, out):
    xs_dram = nc.dram_tensor("moe_in", (EXPERTS * REGION, D), F32, kind="Internal").ap()
    ys_dram = nc.dram_tensor("moe_out", (MOE_TILES * SLOTS, D), F32, kind="Internal").ap()

    ctx = ExitStack()
    with ctx:
        def sb(name, shape, dt=F32):
            return ctx.enter_context(nc.sbuf_tensor(name, shape, dt))

        def pb(name):
            return ctx.enter_context(nc.psum_tensor(name, [P, 2 * GROUP], F32))

        def sem(name):
            return ctx.enter_context(nc.semaphore(name))

        xacc = sb("xacc", [P, TILES, D])
        xnT = sb("xnT", [P, TOKENS])
        xn = sb("xn", [P, TILES * D])
        WinT = sb("WinT", [P, 2 * INNER])
        Wc = sb("Wc", [P, HALVES, INNER])
        WgB = sb("WgB", [P, 4, P])
        WoT = sb("WoT", [P, HALVES, D])
        cw = sb("cw", [P, HALVES, TAPS])
        cb = sb("cb", [P, HALVES])
        bdt = sb("bdt", [P, HALVES])
        dsk = sb("dsk", [P, HALVES])
        dsk8 = sb("dsk8", [P, HALVES])
        wg = sb("wg", [P, EXPERTS])
        ident = sb("ident", [P, P])
        prob = sb("prob", [P, TOP_K, TILES])
        slot_u = sb("slot_u", [P, TOP_K, TILES], U32)
        eid_i = sb("eid_i", [P, MOE_TILES], I32)
        src_i = sb("src_i", [P, MOE_TILES], I32)
        back_u = sb("back_u", [P, TOP_K, TILES], U32)
        pad_i = sb("pad_i", [P, EXPERTS], I32)
        nbdt = sb("nbdt", [P, HALVES])
        bdt05 = sb("bdt05", [P, HALVES])
        zrow = sb("zrow", [P, 1, D])

        acc = sb("acc", [P, HALVES, GROUP])
        xc = sb("xc", [P, SLOT3, HALVES, GROUP])
        sz = sb("sz", [P, SLOT3, HALVES, GROUP])
        ebuf = sb("ebuf", [P, HALVES, GROUP])
        th = sb("th", [P, HALVES, GROUP])
        al = sb("al", [P, HALVES, GROUP])
        gbuf = sb("gbuf", [P, HALVES, GROUP])
        hbuf = sb("hbuf", [P, HALVES, GROUP])
        ybuf = sb("ybuf", [P, HALVES, GROUP])
        y2 = sb("y2", [P, HALVES, GROUP])
        thg = sb("thg", [P, 2, GROUP])

        whi = sb("whi", [P, 2, 2 * HID], F32R)
        wlo = sb("wlo", [P, 2, 2 * HID], F32R)
        xhi = sb("xhi", [P, 2, SLOTS], F32R)
        xlo = sb("xlo", [P, 2, SLOTS], F32R)

        def in_xn(at, n):
            return xn[:, at:at + n]
        w13 = [in_xn(512 * b, 512) for b in range(2)]
        w2b = [in_xn(1024 + 256 * b, 256) for b in range(2)]
        xs = [in_xn(1536 + 512 * b, 512) for b in range(2)]
        sil = in_xn(2560, 1024)
        hid = [in_xn(3584 + 1024 * b, 1024) for b in range(2)]
        yo = [in_xn(5632 + 512 * b, 512) for b in range(2)]
        got = [in_xn(2048 * b, 2048).rearrange("p (g k j d) -> p g k j d", g=2, k=TOP_K, j=GT)
               for b in range(SLOT3)]

        def flat(t):
            return t.rearrange("p a b -> p (a b)")
        win_raw = flat(acc[:, :, :])[:, 0:512].rearrange("p (a b) -> p a b", a=4)
        wdt_raw = flat(acc[:, :, :])[:, 512:1024].rearrange("p (a b) -> p a b", a=2)
        wx_raw = flat(ebuf[:, :, :])[:, 0:512].rearrange("p (a b) -> p a b", a=2)
        wxB = ebuf[0:STATE, 1, 0:256]
        wxC = ebuf[0:STATE, 1, 256:512]
        wo_raw = flat(th[:, :, :])[:, 0:256]
        wdtT = flat(th[:, :, :])[:, 512:1024].rearrange("p (a b) -> p a b", a=2)
        inv16 = th[0:STATE, 0, 256:256 + P]
        ones_pp = flat(al[:, :, :])[:, 0:128]
        tri = flat(al[:, :, :])[:, 128:256]
        iot = flat(al[:, :, :])[:, 256:640].bitcast(I32)
        ones64 = flat(al[:, :, :])[:, 640:704]
        thr = flat(al[:, :, :])[:, 704:832].rearrange("p (e m) -> p e m", e=EXPERTS)
        rev = flat(al[:, :, :])[:, 832:840]
        tix = flat(al[:, :, :])[:, 840:840 + MOE_TILES]
        nte = flat(al[:, :, :])[:, 896:904]
        nti = flat(al[:, :, :])[:, 904:912]
        reg0 = flat(al[:, :, :])[:, 912:920]
        eid_f = flat(al[:, :, :])[:, 920:920 + MOE_TILES]
        row_f = flat(al[:, :, :])[:, 960:960 + MOE_TILES]
        skip = flat(al[:, :, :])[:, 1000:1008]
        pad_f = flat(al[:, :, :])[:, 1008:1016]
        move = flat(al[:, :, :])[:, 1016:1024]
        st = flat(gbuf[:, :, :])[:, 0:QT * 6].rearrange("p (j s) -> p j s", s=6)
        mv = flat(gbuf[:, :, :])[:, 128:128 + QT * 2].rearrange("p (j s) -> p j s", s=2)
        var = flat(gbuf[:, :, :])[:, 192:192 + QT]
        std = flat(gbuf[:, :, :])[:, 224:224 + QT]
        rst = flat(gbuf[:, :, :])[:, 256:256 + QT]
        nrt = flat(gbuf[:, :, :])[:, 288:288 + QT]

        def je(t):
            return t.rearrange("p (j e) -> p j e", e=EXPERTS)
        L = je(hbuf[:, 0, :])
        L2 = je(hbuf[:, 1, :])
        oh1 = je(ybuf[:, 0, :])
        oh2 = je(ybuf[:, 1, :])
        msk = je(y2[:, 0, :])
        tmp = je(y2[:, 1, :])
        tot = je(sz[:, 2, 0, :])
        inc = je(sz[:, 2, 1, :])
        m1 = gbuf[:, 1, 0:64]
        m2 = gbuf[:, 1, 64:128]
        c1 = gbuf[:, 1, 128:192]
        sf = gbuf[:, 1, 192:320].rearrange("p (k j) -> p k j", k=TOP_K)
        dlt = gbuf[:, 1, 320:384]
        den = gbuf[:, 1, 384:448]
        cmp_m = flat(xc[:, 2, :, :])[:, 0:EXPERTS * 16].rearrange("p (e m) -> p e m", e=EXPERTS)
        cmp_t = flat(xc[:, 2, :, :])[:, 128:128 + MOE_TILES * EXPERTS].rearrange("p (t e) -> p t e", e=EXPERTS)
        cmp_s = flat(xc[:, 2, :, :])[:, 512:512 + MOE_TILES * EXPERTS].rearrange("p (t e) -> p t e", e=EXPERTS)
        tail = flat(xc[:, 2, :, :])[:, 896:896 + MOE_TILES]

        PA, PB, PC, PD = pb("PA"), pb("PB"), pb("PC"), pb("PD")

        s_x = [sem(f"s_x_{q}") for q in range(QUARTERS)]
        s_wg = sem("s_wg")
        s_wld = sem("s_wld")
        s_zrow = sem("s_zrow")
        s_fill = sem("s_fill")
        s_cst = sem("s_cst")
        s_wtp = sem("s_wtp")
        s_wcp = sem("s_wcp")
        s_dve = sem("s_dve")
        s_var = sem("s_var")
        s_std = sem("s_std")
        s_xn = sem("s_xn")
        s_xt = sem("s_xt")
        s_xnT = sem("s_xnT")
        s_lg = sem("s_lg")
        s_lcp = sem("s_lcp")
        s_msk = sem("s_msk")
        s_rk = sem("s_rk")
        s_dlt = sem("s_dlt")
        s_edl = sem("s_edl")
        s_slot = sem("s_slot")
        s_eid = sem("s_eid")
        s_back = sem("s_back")
        s_scat = sem("s_scat")
        s_xp = sem("s_xp")
        s_z = sem("s_z")
        s_tap0 = sem("s_tap0")
        s_taps = sem("s_taps")
        s_cv = sem("s_cv")
        s_xc = sem("s_xc")
        s_sz = sem("s_sz")
        s_u = sem("s_u")
        s_g = sem("s_g")
        s_abs = sem("s_abs")
        s_exp = sem("s_exp")
        s_ln = sem("s_ln")
        s_dt = sem("s_dt")
        s_th = sem("s_th")
        s_al = sem("s_al")
        s_thg = sem("s_thg")
        s_ch = sem("s_ch")
        s_y2 = sem("s_y2")
        s_out = sem("s_out")
        s_add = sem("s_add")
        s_w13 = [sem(f"s_w13_{b}") for b in range(2)]
        s_w2 = [sem(f"s_w2_{b}") for b in range(2)]
        s_xs = [sem(f"s_xs_{b}") for b in range(2)]
        s_ys = [sem(f"s_ys_{b}") for b in range(2)]
        s_whi = sem("s_whi")
        s_wlo = sem("s_wlo")
        s_T = sem("s_T")
        s_xhi = sem("s_xhi")
        s_xlo = sem("s_xlo")
        s_h1 = sem("s_h1")
        s_h3 = sem("s_h3")
        s_sil = sem("s_sil")
        s_hid = sem("s_hid")
        s_y = sem("s_y")
        s_yc = sem("s_yc")
        s_got = [sem(f"s_got_{b}") for b in range(SLOT3)]
        s_comb = sem("s_comb")
        s_ch2 = sem("s_ch2")
        s_store = sem("s_store")

        x_q = x.rearrange("b l d -> (b l) d").rearrange("(q j p) d -> q p j d", q=QUARTERS, p=P)
        out_t = out.rearrange("b l d -> (b l) d").rearrange("(j p) d -> p j d", p=P)

        ys_tile = ys_dram.rearrange("(t j p) d -> p t j d", p=P, j=GT)

        ctx.enter_context(nc.allow_non_contiguous_dma(reason="three vectors of 256 elements"))
        block = ctx.enter_context(nc.Block())

        def mixer(eng, step, first, last, extra=None):
            def whole(g):
                step(g, g % SLOT3, g + 1 < GROUPS, 0 <= g < GROUPS, 1 <= g <= GROUPS, g >= 2)
                if extra:
                    extra(g, None)
            start = max(first, 2)
            for g in range(first, min(start, last)):
                whole(g)
            turns = max(min(last, GROUPS - 1) - start, 0) // SLOT3
            if turns:
                with eng.Fori(0, turns) as i:
                    for k in range(SLOT3):
                        step(i * SLOT3 + (start + k), (start + k) % SLOT3, True, True, True, True)
                        if extra:
                            extra(i * SLOT3 + (start + k), (i, start + k))
            for g in range(start + turns * SLOT3, last):
                whole(g)

        @block.sync
        def _(sp):
            for q in range(QUARTERS):
                sp.dma_start(xacc[:, q * QT:(q + 1) * QT, :], x_q[q]).then_inc(s_x[q], 16)
                if q == 0:
                    sp.dma_start(wg[:, :], w_gate).then_inc(s_wg, 16)
            sp.dma_start(win_raw, W_in.rearrange("(a p) h -> p a h", p=P)).then_inc(s_wld, 16)
            sp.dma_start(wdt_raw, W_dt.rearrange("(a p) k -> p a k", p=P)).then_inc(s_wld, 16)
            sp.dma_start(wx_raw, W_x[2 * STATE:, :].rearrange("(a p) i -> p a i", p=P)).then_inc(s_wld, 16)
            sp.dma_start(wxB, W_x[0:STATE, :]).then_inc(s_wld, 16)
            sp.dma_start(wxC, W_x[STATE:2 * STATE, :]).then_inc(s_wld, 16)
            sp.dma_start(wo_raw, W_out).then_inc(s_wld, 16)
            sp.dma_start(cw[:, :, :], conv_w.rearrange("(c p) o k -> p c (o k)", p=P)).then_inc(s_wld, 16)
            sp.dma_start(cb[:, :], conv_b.rearrange("(c p) -> p c", p=P)).then_inc(s_wld, 16)
            sp.dma_start(bdt[:, :], b_dt.rearrange("(c p) -> p c", p=P)).then_inc(s_wld, 16)
            sp.dma_start(dsk[:, :], D_skip.rearrange("(c p) -> p c", p=P)).then_inc(s_wld, 16)
            def entry(table, t, last):
                at = slice(t, t + 1) if isinstance(t, int) else bass.ds(t, 1)
                return sp.value_load(table[0:1, at], min_val=0, max_val=last)

            def load_up(t, b, first):
                e = entry(eid_i, t, EXPERTS - 1)
                row = entry(src_i, t, EXPERTS * REGION - SLOTS)
                if not first:
                    sp.wait_ge(s_whi, t - 1)
                    sp.wait_ge(s_wlo, t - 1)
                dst = w13[b].rearrange("p (a h) -> p a h", a=2)
                sp.dma_start(dst[:, 0, :], w1[bass.ds(e, 1)].rearrange("e d h -> d (e h)")).then_inc(s_w13[b], 16)
                sp.dma_start(dst[:, 1, :], w3[bass.ds(e, 1)].rearrange("e d h -> d (e h)")).then_inc(s_w13[b], 16)
                if not first:
                    sp.wait_ge(s_T, t - 1)
                sp.dma_start(xs[b].rearrange("p (j d) -> p j d", j=GT),
                             xs_dram[bass.ds(row, SLOTS), :].rearrange("(j p) d -> p j d", p=P)).then_inc(s_xs[b], 16)

            def load_down(t, b, first):
                e = entry(eid_i, t, EXPERTS - 1)
                if not first:
                    sp.wait_ge(s_y, t - 1)
                sp.dma_start(w2b[b].rearrange("p (o k d) -> p o k d", o=1, k=HALVES),
                             w2[bass.ds(e, 1)].rearrange("e (k p) d -> p e k d", p=P)).then_inc(s_w2[b], 16)

            def store(t, b):
                sp.wait_ge(s_yc, t + 1)
                dst = ys_tile[:, t:t + 1] if isinstance(t, int) else ys_tile[:, bass.ds(t, 1)]
                sp.dma_start(dst, yo[b].rearrange("p (o j d) -> p o j d", o=1, j=GT)).then_inc(s_ys[b], 16)

            sp.wait_ge(s_eid, 1)
            sp.wait_ge(s_zrow, 1)
            for e in range(EXPERTS):
                row = entry(pad_i, e, EXPERTS * REGION - SLOTS)
                sp.dma_start(xs_dram[bass.ds(row, SLOTS), :].rearrange("(j p) d -> p j d", p=P),
                             zrow[:, :, :].broadcast_to([P, GT, D])).then_inc(s_fill, 16)
            sp.wait_ge(s_fill, 16 * EXPERTS)
            sp.wait_ge(s_scat, 16 * TOP_K * TILES)
            load_up(0, 0, True)
            load_down(0, 0, True)
            load_up(1, 1, True)
            load_down(1, 1, True)
            load_up(2, 0, False)
            load_up(3, 1, False)
            with sp.Fori(0, (MOE_TILES - 5) // 2) as i:
                load_down(i * 2 + 2, 0, False)
                store(i * 2, 0)
                load_up(i * 2 + 4, 0, False)
                load_down(i * 2 + 3, 1, False)
                store(i * 2 + 1, 1)
                load_up(i * 2 + 5, 1, False)
            t = MOE_TILES - 3
            load_down(t, 0, False)
            store(t - 2, 0)
            load_up(t + 2, 0, False)
            load_down(t + 1, 1, False)
            store(t - 1, 1)
            load_down(t + 2, 0, False)
            for t in range(MOE_TILES - 3, MOE_TILES):
                store(t, t % 2)

            for k in range(GROUPS // 2):
                sp.wait_ge(s_add, 2 * k + 3)
                sp.wait_ge(s_comb, k + 1)
                at = slice(2 * k * GT, (2 * k + 2) * GT)
                sp.dma_start(out_t[:, at], xacc[:, at]).then_inc(s_store, 16)
            sp.wait_ge(s_store, 16 * (GROUPS // 2))

        @block.gpsimd
        def _(gp):
            gp.memset(ident[:, :], 0.0).then_inc(s_cst, 1)
            gp.memset(tri, 0.0).then_inc(s_cst, 1)
            gp.memset(ones_pp, 1.0).then_inc(s_cst, 1)
            gp.memset(inv16, 1.0 / STATE).then_inc(s_cst, 1)
            gp.memset(ones64, 1.0).then_inc(s_cst, 1)
            gp.iota(iot[:, 0:128], [[0, EXPERTS], [SLOTS, 16]], base=0, channel_multiplier=0).then_inc(s_cst, 1)
            gp.iota(iot[:, 128:128 + EXPERTS], [[-1, EXPERTS]], base=EXPERTS, channel_multiplier=0).then_inc(s_cst, 1)
            gp.iota(iot[:, 256:256 + MOE_TILES], [[1, MOE_TILES]], base=0, channel_multiplier=0).then_inc(s_cst, 1)
            gp.iota(iot[:, 320:320 + EXPERTS], [[REGION, EXPERTS]], base=0, channel_multiplier=0).then_inc(s_cst, 1)
            gp.wait_ge(s_cst, 9)
            gp.affine_select(out=ident[:, :], in_=ident[:, :], compare_op=ALU.not_equal, fill=1.0,
                             base=0, pattern=[[-1, P]], channel_multiplier=1).then_inc(s_cst, 1)
            gp.affine_select(out=tri, in_=tri, compare_op=ALU.is_ge, fill=1.0,
                             base=0, pattern=[[-1, P]], channel_multiplier=1).then_inc(s_cst, 1)
            for n, (q0, qn) in enumerate(CHUNKS):
                gp.wait_ge(s_slot, n + 1)
                for j in range(q0 * QT, (q0 + qn) * QT):
                    for k in range(TOP_K):
                        gp.indirect_dma_start(xs_dram, bass.IndirectOffsetOnAxis(ap=slot_u[:, k, j:j + 1], axis=0),
                                              xn[:, j * D:(j + 1) * D], None).then_inc(s_scat, 16)

            def step(t, n, b, more):
                gp.wait_ge(s_whi, t + 1)
                if not (isinstance(t, int) and t < 2):
                    gp.wait_ge(s_h3, t - 1)
                gp.tensor_tensor(wlo[:, b, :], w13[b], whi[:, b, :].bitcast(F32), ALU.subtract).then_inc(s_wlo, 1)
            step(0, 0, 0, True)
            step(1, 0, 1, True)
            with gp.Fori(0, (MOE_TILES - 3) // 2) as i:
                step(i * 2 + 2, i + 1, 0, True)
                step(i * 2 + 3, i + 1, 1, True)
            step(MOE_TILES - 1, 0, 0, False)

            gp.wait_ge(s_ys[0], 16 * ((MOE_TILES + 1) // 2))
            gp.wait_ge(s_ys[1], 16 * (MOE_TILES // 2))
            for k in range(GROUPS // 2):
                if k >= SLOT3:
                    gp.wait_ge(s_comb, k - SLOT3 + 1)
                for g in range(2):
                    for c in range(TOP_K):
                        for j in range(GT):
                            tile = (2 * k + g) * GT + j
                            gp.indirect_dma_start(
                                got[k % SLOT3][:, g, c, j, :], None, ys_dram,
                                bass.IndirectOffsetOnAxis(ap=back_u[:, c, tile:tile + 1], axis=0),
                            ).then_inc(s_got[k % SLOT3], 16)

        @block.tensor
        def _(pe):
            def setup(r):
                if r == 0:
                    pe.wait_ge(s_wld, 16 * 10)
                    for a in range(4):
                        pe.transpose(PB[:, a * P:(a + 1) * P], win_raw[:, a, :], ident[:, :])
                    for kb in range(2):
                        for ob in range(2):
                            at = 512 + kb * 256 + ob * 128
                            last = pe.transpose(PB[:, at:at + P], wdt_raw[:, ob, kb * P:(kb + 1) * P], ident[:, :])
                elif r == 1:
                    pe.wait_ge(s_wcp, 2)
                    for ib in range(2):
                        pe.transpose(PB[:, ib * P:(ib + 1) * P], wo_raw[:, ib * P:(ib + 1) * P], ident[:, :])
                    for n, rows in enumerate((wxB, wxC)):
                        for ib in range(2):
                            at = 512 + (n * 2 + ib) * P
                            last = pe.matmul(PB[:, at:at + P], rows[:, ib * P:(ib + 1) * P], inv16, start=True, stop=True)
                else:
                    pe.wait_ge(s_wcp, 4)
                    for ib in range(2):
                        for kb in range(2):
                            last = pe.matmul(PB[:, ib * 256:(ib + 1) * 256], wx_raw[:, kb, ib * P:(ib + 1) * P],
                                             wdtT[:, kb, :], start=(kb == 0), stop=(kb == 1))
                last.then_inc(s_wtp, 1)

            pe.wait_ge(s_cst, 11)
            pe.wait_ge(s_wg, 16)
            def logits(g):
                pe.wait_ge(s_xnT, g + 1)
                q = g * GT // QT
                if q >= 2:
                    pe.wait_ge(s_lcp, q - 1)
                for j in range(GT * g, GT * g + GT):
                    at = (q + 1) % 2 * 512 + j * EXPERTS
                    last = pe.matmul(PC[:, at:at + EXPERTS], xnT[:, j * P:(j + 1) * P],
                                     wg[:, :], start=True, stop=True)
                last.then_inc(s_lg, 1)

            def ranks(n):
                q0, qn = CHUNKS[n]
                pe.wait_ge(s_msk, n + 1)
                m = msk[:, q0 * QT:(q0 + qn) * QT, :].rearrange("p j e -> p (j e)")
                at, to = q0 * QT * EXPERTS, (q0 + qn) * QT * EXPERTS
                pe.matmul(PD[:, at:to], tri, m, start=True, stop=True).then_inc(s_rk, 1)
                pe.matmul(PD[:, 512 + at:512 + to], ones_pp, m, start=True, stop=True).then_inc(s_rk, 1)

            def mix(g, slot, a, b, c, d):
                static = isinstance(g, int)
                if a:
                    src = xnT[:, bass.ds(g * GROUP + GROUP, GROUP)] if not static else \
                        xnT[:, (g + 1) * GROUP:(g + 2) * GROUP]
                    if not (static and g + 1 < 1):
                        pe.wait_ge(s_taps, g + 1)
                    for c_ in range(HALVES):
                        last = pe.matmul(PA[:, c_ * GROUP:(c_ + 1) * GROUP], WinT[:, c_ * P:(c_ + 1) * P], src,
                                         start=True, stop=True)
                    last.then_inc(s_xp, 1)
                if d:
                    pe.wait_ge(s_y2, g - 1)
                    if b:
                        pe.wait_ge(s_sz, g + 1)
                    else:
                        pe.wait_ge(s_add, g - 1)
                    for j in range(GT):
                        for k in range(HALVES):
                            last = pe.matmul(PB[:, j * D:(j + 1) * D], y2[:, k, j * P:(j + 1) * P], WoT[:, k, :],
                                             start=(k == 0), stop=(k == 1))
                    last.then_inc(s_out, 1)
                if b:
                    pe.wait_ge(s_xc, g + 1)
                    if not (static and g < 1):
                        pe.wait_ge(s_dt, g)
                    else:
                        pe.wait_ge(s_lcp, QUARTERS)
                    for c_ in range(HALVES):
                        for k in range(HALVES):
                            last = pe.matmul(PC[:, c_ * GROUP:(c_ + 1) * GROUP], Wc[:, k, c_ * P:(c_ + 1) * P],
                                             xc[:, slot, k, :], start=(k == 0), stop=(k == 1))
                    last.then_inc(s_u, 1)
                if a:
                    if not (static and g + 1 < 1):
                        pe.wait_ge(s_sz, g + 1)
                    if d:
                        pe.wait_ge(s_add, g)
                    for c_ in range(HALVES):
                        last = pe.matmul(PB[:, c_ * GROUP:(c_ + 1) * GROUP],
                                         WinT[:, INNER + c_ * P:INNER + (c_ + 1) * P], src, start=True, stop=True)
                    last.then_inc(s_z, 1)
                if b:
                    if not (static and g < 1):
                        pe.wait_ge(s_thg, g)
                    else:
                        pe.wait_ge(s_slot, len(CHUNKS))
                    if static and g == STEPS_A:
                        pe.wait_ge(s_yc, MOE_TILES)
                    for n in range(2):
                        for k in range(HALVES):
                            last = pe.matmul(PD[:, n * GROUP:(n + 1) * GROUP], WgB[:, n * 2 + k, :],
                                             xc[:, slot, k, :], start=(k == 0), stop=(k == 1))
                    last.then_inc(s_g, 1)

            for g in range(GROUPS):
                pe.wait_ge(s_xn, g + 1)
                if g >= 2:
                    pe.wait_ge(s_xnT, g - 1)
                for j in range(GT):
                    t = g * GT + j
                    at = (g % 2) * 512 + j * P
                    last = pe.transpose(PA[:, at:at + P], xn[:, t * D:(t + 1) * D], ident[:, :])
                last.then_inc(s_xt, 1)
                if g * GT % QT:
                    logits(g - 1)
                if (g + 1) * GT % QT == 0:
                    logits(g)
                if g in SETUP_AT:
                    setup(SETUP_AT.index(g))
                for n, (q0, qn) in enumerate(CHUNKS):
                    if g == min(q0 + qn + 1, QUARTERS) * QT // GT - 1:
                        if n == len(CHUNKS) - 1:
                            pe.wait_ge(s_xnT, GROUPS)
                            pe.wait_ge(s_wcp, 8)
                            mixer(pe, mix, -1, 0)
                        ranks(n)

            pe.sem_inc(s_out, 1)
            mixer(pe, mix, 0, STEPS_A)

            def transp(t, n, b, first):
                pe.wait_ge(s_xs[b], n * 16 + 16)
                if not first:
                    pe.wait_ge(s_xhi, t)
                    pe.wait_ge(s_xlo, t)
                for j in range(GT):
                    last = pe.transpose(PD[:, j * P:(j + 1) * P], xs[b][:, j * D:(j + 1) * D], ident[:, :])
                last.then_inc(s_T, 1)

            def up(t, b, first):
                pe.wait_ge(s_wlo, t + 1)
                pe.wait_ge(s_xhi, t + 1)
                for m, (ps, free, done) in enumerate(((PA, s_sil, s_h1), (PB, s_hid, s_h3))):
                    if not first:
                        pe.wait_ge(free, t)
                    for c_ in range(HALVES):
                        at = m * HID + c_ * P
                        o = ps[:, c_ * SLOTS:(c_ + 1) * SLOTS]
                        pe.matmul(o, whi[:, b, at:at + P], xhi[:, b, :], start=True, stop=False)
                        pe.matmul(o, wlo[:, b, at:at + P], xhi[:, b, :], start=False, stop=False)
                        pe.wait_ge(s_xlo, t + 1)
                        last = pe.matmul(o, whi[:, b, at:at + P], xlo[:, b, :], start=False, stop=True)
                    last.then_inc(done, 1)

            def down(t, n, b, first):
                pe.wait_ge(s_hid, t + 1)
                pe.wait_ge(s_w2[b], n * 16 + 16)
                if not first:
                    pe.wait_ge(s_yc, t)
                for j in range(GT):
                    for k in range(HALVES):
                        last = pe.matmul(PD[:, 512 + j * D:512 + (j + 1) * D],
                                         hid[b][:, k * SLOTS + j * P:k * SLOTS + (j + 1) * P],
                                         w2b[b][:, k * D:(k + 1) * D], start=(k == 0), stop=(k == 1))
                last.then_inc(s_y, 1)

            pe.wait_ge(s_thg, STEPS_A)
            pe.wait_ge(s_taps, STEPS_A + 1)
            pe.wait_ge(s_sz, STEPS_A + 1)
            pe.wait_ge(s_add, STEPS_A - 1)
            transp(0, 0, 0, True)
            up(0, 0, True)
            transp(1, 0, 1, False)
            up(1, 1, False)
            transp(2, 1, 0, False)
            down(0, 0, 0, True)
            with pe.Fori(0, (MOE_TILES - 3) // 2) as i:
                up(i * 2 + 2, 0, False)
                transp(i * 2 + 3, i + 1, 1, False)
                down(i * 2 + 1, i, 1, False)
                up(i * 2 + 3, 1, False)
                transp(i * 2 + 4, i + 2, 0, False)
                down(i * 2 + 2, i + 1, 0, False)
            t = MOE_TILES - 1
            up(t, 0, False)
            down(t - 1, (t - 1) // 2, 1, False)
            down(t, t // 2, 0, False)

            pe.wait_ge(s_sil, MOE_TILES)
            pe.wait_ge(s_hid, MOE_TILES)
            mixer(pe, mix, STEPS_A, FIRST_PAIR)
            mixer(pe, mix, FIRST_PAIR, GROUPS + 2)

        @block.scalar
        def _(act):
            act.preload_act_table_set("sqrt_and_others")
            def setup(r):
                act.wait_ge(s_wtp, r + 1)
                if r == 0:
                    act.activation(WinT[:, :], PB[:, 0:512], ACT.Copy).then_inc(s_wcp, 1)
                    act.activation(wdtT, PB[:, 512:1024].rearrange("p (a b) -> p a b", a=2), ACT.Copy).then_inc(s_wcp, 1)
                elif r == 1:
                    act.activation(WoT[:, :, :], PB[:, 0:256].rearrange("p (a b) -> p a b", a=2), ACT.Copy,
                                   scale=-0.125).then_inc(s_wcp, 1)
                    act.activation(WgB[:, :, :], PB[:, 512:1024].rearrange("p (a b) -> p a b", a=4),
                                   ACT.Copy).then_inc(s_wcp, 1)
                else:
                    act.activation(Wc[:, :, :], PB[:, 0:512].rearrange("p (a b) -> p a b", a=2),
                                   ACT.Copy).then_inc(s_wcp, 1)
                    act.activation(dsk8[:, :], dsk[:, :], ACT.Copy, scale=-8.0).then_inc(s_wcp, 1)
                    act.activation(nbdt[:, :], bdt[:, :], ACT.Copy, scale=-1.0).then_inc(s_wcp, 1)
                    act.activation(bdt05[:, :], bdt[:, :], ACT.Copy, scale=0.05).then_inc(s_wcp, 1)

            for q in range(QUARTERS):
                act.wait_ge(s_var, q + 1)
                act.activation(std, var, ACT.Sqrt).then_inc(s_std, 1)
                for g in range(q * GROUPS // QUARTERS, (q + 1) * GROUPS // QUARTERS):
                    act.wait_ge(s_xt, g + 1)
                    act.activation(xnT[:, g * GROUP:(g + 1) * GROUP], PA[:, (g % 2) * 512:(g % 2) * 512 + 512],
                                   ACT.Copy).then_inc(s_xnT, 1)
                    if g - 1 in SETUP_AT:
                        setup(SETUP_AT.index(g - 1))
            def mix(g, slot, a, b, c, d):
                static = isinstance(g, int)
                nxt = (slot + 1) % SLOT3
                if not (b or c):
                    act.preload_act_table_set("silu_and_others")
                if a:
                    act.wait_ge(s_xp, g + 2)
                    if not (static and g + 1 < 1):
                        act.wait_ge(s_xc, g + 1)
                    for c_ in range(HALVES):
                        last = act.activation(acc[:, c_, :], PA[:, c_ * GROUP:(c_ + 1) * GROUP], ACT.Identity,
                                              bias=cb[:, c_:c_ + 1], scale=cw[:, c_, TAPS - 1:TAPS])
                    last.then_inc(s_tap0, 1)
                if c:
                    act.wait_ge(s_dt, g)
                    if not (static and g < 2):
                        act.wait_ge(s_ch, g * CHAIN - 2 * CHAIN + 1)
                    for c_ in range(HALVES):
                        last = act.activation(th[:, c_, :], ebuf[:, c_, :], ACT.Tanh, scale=0.05,
                                              bias=bdt05[:, c_:c_ + 1])
                    last.then_inc(s_th, 1)
                    act.wait_ge(s_th, g)
                    if not (static and g < 2):
                        act.wait_ge(s_ch, g * CHAIN - 2 * CHAIN + 5)
                    act.activation(al[:, :, :], th[:, :, :], ACT.Copy, bias=0.5, scale=0.5).then_inc(s_al, 1)
                if b:
                    act.preload_act_table_set("natural_log_exp_and_others")
                    act.wait_ge(s_u, g + 1)
                    if not (static and g < 1):
                        act.wait_ge(s_th, g)
                    for c_ in range(HALVES):
                        last = act.activation(ebuf[:, c_, :], PC[:, c_ * GROUP:(c_ + 1) * GROUP], ACT.Abs,
                                              bias=bdt[:, c_:c_ + 1])
                    last.then_inc(s_abs, 1)
                    act.wait_ge(s_abs, g + 1)
                    act.activation(ebuf[:, :, :], ebuf[:, :, :], ACT.Exp, scale=-1.0).then_inc(s_exp, 1)
                    act.wait_ge(s_exp, g + 1)
                    act.activation(ebuf[:, :, :], ebuf[:, :, :], ACT.Ln, bias=1.0).then_inc(s_ln, 1)
                    act.preload_act_table_set("silu_and_others")
                if a:
                    act.wait_ge(s_z, g + 2)
                    act.activation(sz[:, nxt].rearrange("p a b -> p (a b)"), PB[:, :], ACT.Silu).then_inc(s_sz, 1)
                if b:
                    act.wait_ge(s_g, g + 1)
                    if c:
                        act.wait_ge(s_ch, g * CHAIN - CHAIN + 6)
                    act.activation(thg[:, :, :].rearrange("p a b -> p (a b)"), PD[:, :], ACT.Tanh,
                                   scale=0.5).then_inc(s_thg, 1)
                if a:
                    act.wait_ge(s_taps, g + 2)
                    act.activation(xc[:, nxt], acc[:, :, :], ACT.Silu).then_inc(s_xc, 1)

            mixer(act, mix, -1, 0)
            act.preload_act_table_set("natural_log_exp_and_others")
            act.wait_ge(s_dlt, 1)
            act.activation(den, dlt, ACT.Exp).then_inc(s_edl, 1)
            mixer(act, mix, 0, 1)
            act.wait_ge(s_back, 1)
            mixer(act, mix, 1, STEPS_A)

            def round_w(t, n, b, first):
                act.wait_ge(s_w13[b], n * 32 + 32)
                if not first:
                    act.wait_ge(s_h3, t - 1)
                act.activation(whi[:, b, :], w13[b], ACT.Copy).then_inc(s_whi, 1)

            def round_x(t, b):
                act.wait_ge(s_T, t + 1)
                act.activation(xhi[:, b, :], PD[:, 0:512], ACT.Copy).then_inc(s_xhi, 1)

            def gate(t, first):
                act.wait_ge(s_h1, t + 1)
                if not first:
                    act.wait_ge(s_hid, t)
                act.activation(sil, PA[:, :], ACT.Silu).then_inc(s_sil, 1)

            def copy_y(t, n, b, first):
                act.wait_ge(s_y, t + 1)
                if not first:
                    act.wait_ge(s_ys[b], n * 16)
                act.activation(yo[b], PD[:, 512:1024], ACT.Copy).then_inc(s_yc, 1)

            def tile_step(t, n, b, more):
                if more:
                    round_w(t + 1, n + b, 1 - b, False)
                gate(t, False)
                if more:
                    round_x(t + 1, 1 - b)
                copy_y(t - 1, n + b - 1, 1 - b, False)

            round_w(0, 0, 0, True)
            round_x(0, 0)
            round_w(1, 0, 1, True)
            gate(0, True)
            round_x(1, 1)
            round_w(2, 1, 0, False)
            gate(1, False)
            round_x(2, 0)
            copy_y(0, 0, 0, True)
            round_w(3, 1, 1, False)
            gate(2, False)
            round_x(3, 1)
            copy_y(1, 0, 1, True)
            with act.Fori(0, (MOE_TILES - 5) // 2) as i:
                tile_step(i * 2 + 3, i + 1, 1, True)
                tile_step(i * 2 + 4, i + 2, 0, True)
            t = MOE_TILES - 2
            tile_step(t, t // 2, 1, True)
            tile_step(t + 1, (t + 1) // 2, 0, False)
            copy_y(t + 1, (t + 1) // 2, 0, False)

            mixer(act, mix, STEPS_A, FIRST_PAIR)
            mixer(act, mix, FIRST_PAIR, GROUPS + 2)

        @block.vector
        def _(ve):
            count = [0]

            def link(ins):
                count[0] += 1
                ins.then_inc(s_dve, 1)
                ve.wait_ge(s_dve, count[0])

            ve.memset(zrow[:, :, :], 0.0).then_inc(s_zrow, 1)
            ve.sem_inc(s_add, 1)

            def norm(q):
                ve.wait_ge(s_x[q], 16)
                for j in range(QT):
                    last = ve.bn_stats(st[:, j, :], xacc[:, q * QT + j, :])
                link(last)
                for j in range(QT):
                    last = ve.bn_aggr(mv[:, j, :], st[:, j, :])
                link(last)
                ve.tensor_scalar(var, mv[:, :, 1], EPS, None, ALU.add).then_inc(s_var, 1)
                ve.wait_ge(s_var, q + 1)
                ve.wait_ge(s_std, q + 1)
                link(ve.reciprocal(rst, std))
                link(ve.tensor_tensor(nrt, rst, rst, ALU.mult))
                link(ve.tensor_tensor(nrt, nrt, var, ALU.mult))
                link(ve.tensor_scalar(nrt, nrt, -0.5, 1.5, ALU.mult, ALU.add))
                link(ve.tensor_tensor(rst, rst, nrt, ALU.mult))
                for j in range(QT):
                    t = q * QT + j
                    last = ve.tensor_scalar(xn[:, t * D:(t + 1) * D], xacc[:, t, :], mv[:, j, 0:1], rst[:, j:j + 1],
                                            ALU.subtract, ALU.mult)
                    if j % GT == GT - 1:
                        last.then_inc(s_xn, 1)
                ve.wait_ge(s_xn, (q + 1) * QT // GT)

            def pick(logit, best, oh, t_, c_, shape):
                rev_b = rev.unsqueeze(1).broadcast_to(shape)
                link(ve.reduce_max(best, logit, AX_X))
                link(ve.tensor_tensor(t_, logit, best.unsqueeze(2).broadcast_to(shape), ALU.is_equal))
                link(ve.tensor_tensor(t_, t_, rev_b, ALU.mult))
                link(ve.reduce_max(c_, t_, AX_X))
                link(ve.tensor_tensor(oh, rev_b, c_.unsqueeze(2).broadcast_to(shape), ALU.is_equal))

            def take_logits(q):
                ve.wait_ge(s_lg, (q + 1) * QT // GT)
                at, Q = (q + 1) % 2 * 512, slice(q * QT, (q + 1) * QT)
                ve.tensor_copy(L[:, Q, :], je(PC[:, at:at + 512])[:, Q, :]).then_inc(s_lcp, 1)

            def chunk(n):
                q0, qn = CHUNKS[n]
                return q0 * QT, qn * QT, slice(q0 * QT, (q0 + qn) * QT)

            def choose(n):
                j0, jn, J = chunk(n)
                shape = [P, jn, EXPERTS]
                ve.wait_ge(s_lcp, (j0 + jn) // QT)
                pick(L[:, J, :], m1[:, J], oh1[:, J, :], tmp[:, J, :], c1[:, J], shape)
                link(ve.scalar_tensor_tensor(L2[:, J, :], oh1[:, J, :], -3.0e38, L[:, J, :], ALU.mult, ALU.add))
                pick(L2[:, J, :], m2[:, J], oh2[:, J, :], tmp[:, J, :], c1[:, J], shape)
                ve.tensor_tensor(msk[:, J, :], oh1[:, J, :], oh2[:, J, :], ALU.add).then_inc(s_msk, 1)

            def place(n):
                j0, jn, J = chunk(n)
                shape = [P, jn, EXPERTS]
                ve.wait_ge(s_rk, 2 * n + 2)
                link(ve.tensor_copy(tot[:, J, :], je(PD[:, 512:1024])[:, J, :]))
                for e in range(EXPERTS):
                    before = inc[:, j0 - 1, e:e + 1] if j0 else 0.0
                    last = ve.tensor_tensor_scan(inc[:, J, e], ones64[:, 0:jn], tot[:, J, e], before, ALU.mult, ALU.add)
                link(last)
                link(ve.tensor_tensor(tmp[:, J, :], inc[:, J, :], tot[:, J, :], ALU.subtract))
                link(ve.tensor_tensor(tmp[:, J, :], tmp[:, J, :], je(PD[:, 0:512])[:, J, :], ALU.add))
                link(ve.tensor_tensor(tmp[:, J, :], tmp[:, J, :], reg0.unsqueeze(1).broadcast_to(shape), ALU.add))
                for k, oh in enumerate((oh1, oh2)):
                    link(ve.tensor_tensor(L2[:, J, :], oh[:, J, :], tmp[:, J, :], ALU.mult))
                    link(ve.reduce_sum(sf[:, k, J], L2[:, J, :], AX_X))
                ve.tensor_copy(slot_u[:, :, J], sf[:, :, J]).then_inc(s_slot, 1)

            def mix(g, slot, a, b, c, d):
                static = isinstance(g, int)
                prv = (slot + 2) % SLOT3

                def step(ins):
                    ins.then_inc(s_ch, 1)

                def after(n):
                    ve.wait_ge(s_ch, g * CHAIN - CHAIN + n)

                def tap(j, c_):
                    if not a:
                        return
                    if c_ == 0:
                        if j == 1:
                            ve.wait_ge(s_tap0, g + 2)
                        else:
                            ve.wait_ge(s_cv, g * 2 + j + 1)
                    a_v = acc[:, c_, :].rearrange("p (s l) -> p s l", s=SPG)[:, :, j:SEQ]
                    p_v = PA[:, c_ * GROUP:(c_ + 1) * GROUP].rearrange("p (s l) -> p s l", s=SPG)
                    ins = ve.scalar_tensor_tensor(a_v, p_v[:, :, 0:SEQ - j], cw[:, c_, TAPS - 1 - j:TAPS - j],
                                                  a_v, ALU.mult, ALU.add)
                    if c_ == HALVES - 1:
                        ins.then_inc(s_taps if j == TAPS - 1 else s_cv, 1)

                tap(1, 0)
                tap(1, 1)
                if d:
                    ve.wait_ge(s_out, g)
                    at = bass.ds(g * GT - 2 * GT, GT) if not static else slice((g - 2) * GT, (g - 1) * GT)
                    ve.tensor_tensor(xacc[:, at, :], PB[:, 0:GROUP].rearrange("p (j d) -> p j d", j=GT),
                                     xacc[:, at, :], ALU.add).then_inc(s_add, 1)
                if c:
                    ve.wait_ge(s_th, g)
                    step(ve.scalar_tensor_tensor(gbuf[:, :, :], th[:, :, :], -1.0, xc[:, prv], ALU.add, ALU.mult))
                    ve.wait_ge(s_al, g)
                    step(ve.tensor_scalar(al[:, :, :], al[:, :, :], 0.01, 0.99, ALU.max, ALU.min))
                tap(2, 0)
                if c:
                    after(2)
                    step(ve.memset(al[:, :, :].rearrange("p a (s l) -> p a s l", s=SPG)[:, :, :, 0], 0.0))
                    ve.wait_ge(s_thg, g)
                    step(ve.scalar_tensor_tensor(gbuf[:, :, :], thg[:, 0:1, :].broadcast_to([P, HALVES, GROUP]), 1.0,
                                                 gbuf[:, :, :], ALU.add, ALU.mult))
                tap(2, 1)
                if c:
                    after(4)
                    step(ve.tensor_tensor_scan(hbuf[:, :, :].rearrange("p a b -> p (a b)"),
                                               al[:, :, :].rearrange("p a b -> p (a b)"),
                                               gbuf[:, :, :].rearrange("p a b -> p (a b)"), 0.0, ALU.mult, ALU.add))
                tap(3, 0)
                if c:
                    after(5)
                    step(ve.scalar_tensor_tensor(ybuf[:, :, :], thg[:, 1:2, :].broadcast_to([P, HALVES, GROUP]), 1.0,
                                                 hbuf[:, :, :], ALU.add, ALU.mult))
                tap(3, 1)
                if c:
                    after(6)
                    for c_ in range(HALVES):
                        last = ve.scalar_tensor_tensor(ybuf[:, c_, :], xc[:, prv, c_, :], dsk8[:, c_:c_ + 1],
                                                       ybuf[:, c_, :], ALU.mult, ALU.add)
                    step(last)
                    after(7)
                    ve.wait_ge(s_out, g)
                    ve.tensor_tensor(y2[:, :, :], ybuf[:, :, :], sz[:, prv], ALU.mult).then_inc(s_y2, 1)
                if b:
                    ve.wait_ge(s_ln, g + 1)
                    for c_ in range(HALVES):
                        last = ve.scalar_tensor_tensor(ebuf[:, c_, :], PC[:, c_ * GROUP:(c_ + 1) * GROUP],
                                                       nbdt[:, c_:c_ + 1], ebuf[:, c_, :], ALU.max, ALU.add)
                    last.then_inc(s_dt, 1)

            norm(0)
            ve.wait_ge(s_cst, 11)
            ve.tensor_copy(thr, iot[:, 0:128].rearrange("p (e m) -> p e m", e=EXPERTS))
            ve.tensor_copy(rev, iot[:, 128:128 + EXPERTS])
            ve.tensor_copy(tix, iot[:, 256:256 + MOE_TILES])
            link(ve.tensor_copy(reg0, iot[:, 320:320 + EXPERTS]))
            norm(1)
            take_logits(0)
            choose(0)
            norm(2)
            place(0)
            take_logits(1)
            norm(3)
            take_logits(2)
            take_logits(3)
            choose(1)
            ve.tensor_tensor(dlt, m2, m1, ALU.subtract).then_inc(s_dlt, 1)
            mixer(ve, mix, -1, 0)
            place(1)

            cnt = inc[:, TILES - 1, :]
            link(ve.tensor_tensor(cmp_m, thr, cnt.unsqueeze(2).broadcast_to([P, EXPERTS, 16]), ALU.is_lt))
            link(ve.reduce_sum(nte, cmp_m, AX_X))
            link(ve.tensor_tensor_scan(nti, ones64[:, 0:EXPERTS], nte, 0.0, ALU.mult, ALU.add))
            te = [P, MOE_TILES, EXPERTS]
            link(ve.tensor_scalar(skip, nte, -float(SLOTS), float(REGION), ALU.mult, ALU.add))
            link(ve.tensor_tensor(cmp_t, nti.unsqueeze(1).broadcast_to(te), tix.unsqueeze(2).broadcast_to(te),
                                  ALU.is_le))
            link(ve.reduce_sum(eid_f, cmp_t, AX_X))
            link(ve.tensor_tensor(cmp_s, cmp_t, skip.unsqueeze(1).broadcast_to(te), ALU.mult))
            link(ve.reduce_sum(row_f, cmp_s, AX_X))
            link(ve.scalar_tensor_tensor(row_f, tix, float(SLOTS), row_f, ALU.mult, ALU.add))
            link(ve.tensor_scalar(tail, row_f, float(EXPERTS * REGION), None, ALU.is_lt))
            link(ve.tensor_tensor(row_f, row_f, tail, ALU.mult))
            link(ve.tensor_copy(src_i[:, :], row_f))
            link(ve.tensor_scalar(eid_f, eid_f, float(EXPERTS - 1), None, ALU.min))
            link(ve.tensor_tensor(pad_f, cnt, reg0, ALU.add))
            link(ve.tensor_copy(pad_i[:, :], pad_f))
            ve.tensor_copy(eid_i[:, :], eid_f).then_inc(s_eid, 1)
            mixer(ve, mix, 0, 1)
            link(ve.tensor_tensor(move, nti, nte, ALU.subtract))
            link(ve.scalar_tensor_tensor(move, move, float(SLOTS), reg0, ALU.mult, ALU.subtract))
            for k, oh in enumerate((oh1, oh2)):
                link(ve.tensor_tensor(L2, oh, move.unsqueeze(1).broadcast_to([P, TILES, EXPERTS]), ALU.mult))
                link(ve.reduce_sum(c1, L2, AX_X))
                link(ve.tensor_tensor(sf[:, k, :], sf[:, k, :], c1, ALU.add))
            link(ve.tensor_copy(back_u[:, :, :], sf))
            ve.wait_ge(s_edl, 1)
            link(ve.tensor_scalar(c1, den, 1.0, None, ALU.add))
            link(ve.reciprocal(prob[:, 0, :], c1))
            ve.tensor_tensor(prob[:, 1, :], prob[:, 0, :], den, ALU.mult).then_inc(s_back, 1)
            ve.wait_ge(s_back, 1)
            ve.wait_ge(s_slot, len(CHUNKS))
            ve.wait_ge(s_eid, 1)

            mixer(ve, mix, 1, STEPS_A)

            def low(t, b, first):
                ve.wait_ge(s_xhi, t + 1)
                if not first:
                    ve.wait_ge(s_h3, t - 1)
                ve.tensor_tensor(xlo[:, b, :], PD[:, 0:512], xhi[:, b, :].bitcast(F32), ALU.subtract).then_inc(s_xlo, 1)

            def glu(t, b, first):
                ve.wait_ge(s_h3, t + 1)
                ve.wait_ge(s_sil, t + 1)
                if not first:
                    ve.wait_ge(s_y, t - 1)
                ve.tensor_tensor(hid[b], sil, PB[:, :], ALU.mult).then_inc(s_hid, 1)

            low(0, 0, True)
            glu(0, 0, True)
            low(1, 1, True)
            glu(1, 1, True)
            low(2, 0, False)
            with ve.Fori(0, (MOE_TILES - 3) // 2) as i:
                glu(i * 2 + 2, 0, False)
                low(i * 2 + 3, 1, False)
                glu(i * 2 + 3, 1, False)
                low(i * 2 + 4, 0, False)
            glu(MOE_TILES - 1, 0, False)

            filled = 16 * 2 * TOP_K * GT

            def add_pair(k, slot, full, added):
                ve.wait_ge(s_got[slot], full)
                ve.wait_ge(s_add, added)
                for ch in range(TOP_K):
                    if ch:
                        ve.wait_ge(s_ch2, k + 1)
                    for n in range(2):
                        for j in range(GT):
                            tile = k * (2 * GT) + (n * GT + j)
                            at = slice(tile, tile + 1) if isinstance(tile, int) else bass.ds(tile, 1)
                            dst = xacc[:, at, :].rearrange("p o d -> p (o d)")
                            last = ve.scalar_tensor_tensor(dst, got[slot][:, n, ch, j, :], prob[:, ch, at],
                                                           dst, ALU.mult, ALU.add)
                    last.then_inc(s_comb if ch else s_ch2, 1)

            def combine(g, n):
                if n is None:
                    k = g - FIRST_PAIR if g < GROUPS else GROUPS // 2 - 1
                    if k >= 0 and g != GROUPS:
                        add_pair(k, k % SLOT3, filled * (k // SLOT3 + 1), g)
                else:
                    i, m = n
                    k0 = m - FIRST_PAIR
                    add_pair(i * SLOT3 + k0, k0 % SLOT3, i * filled + filled * (k0 // SLOT3 + 1), g)

            mixer(ve, mix, STEPS_A, FIRST_PAIR)
            mixer(ve, mix, FIRST_PAIR, GROUPS + 2, combine)


_INS = ['L0_attn_x', 'L0_attn_W_in', 'L0_attn_conv_w', 'L0_attn_conv_b', 'L0_attn_W_x', 'L0_attn_W_dt',
        'L0_attn_b_dt', 'L0_attn_A_log', 'L0_attn_D', 'L0_attn_W_out', 'L0_ffn_w_gate', 'L0_ffn_w1',
        'L0_ffn_w3', 'L0_ffn_w2']
_OUTS = [((BATCH, SEQ, D), 'float32')]


def kernel(**inputs):
    import numpy as _np
    import concourse.bacc as _bacc
    from concourse import mybir as _mybir
    from concourse.bass_utils import run_bass_kernel_spmd as _run

    nc = _bacc.Bacc("TRN2", target_bir_lowering=False, num_devices=1)
    arrays, args = {}, []
    for name in _INS:
        a = _np.ascontiguousarray(inputs[name])
        arrays[f"in_{name}_dram"] = a
        args.append(nc.dram_tensor(f"in_{name}_dram", a.shape, _mybir.dt.from_np(a.dtype), kind="ExternalInput").ap())
    for i, (shape, dtype) in enumerate(_OUTS):
        dt = _mybir.dt.from_np(_np.dtype(dtype))
        args.append(nc.dram_tensor(f"out_{i}_dram", shape, dt, kind="ExternalOutput").ap())
    block_kernel(nc, *args)
    r = _run(nc, [arrays], core_ids=[0])
    return r.results[0]["out_0_dram"]
```

```python
import concourse.bass as bass
from concourse import mybir
from contextlib import ExitStack

F32 = mybir.dt.float32
F32R = mybir.dt.float32r
I32 = mybir.dt.int32
U32 = mybir.dt.uint32
ALU = mybir.AluOpType
ACT = mybir.ActivationFunctionType
AX_X = mybir.AxisListType.X

P = 128
BATCH, SEQ, D = 32, 256, 128
TOKENS = BATCH * SEQ
TILES = TOKENS // P
GROUP = 512
GROUPS = TOKENS // GROUP
GT = GROUP // P
SPG = GROUP // SEQ
INNER, STATE, TAPS = 256, 16, 4
HALVES = INNER // P
EXPERTS, HID, TOP_K = 8, 256, 2
SLOTS = 512
PAIRS = TOKENS * TOP_K
MOE_TILES = (PAIRS + EXPERTS * (SLOTS - 1)) // SLOTS
EPS = 1e-5
QUARTERS = 4
FILLED = 16 * 2 * GT
QT = TILES // QUARTERS
ROW = D + EXPERTS
STEPS_A = 7
EXP_CAP = 40.0
SLOT3 = 3
REGION = TOKENS + SLOTS
CHUNKS = ((0, 1), (1, 2), (3, 1))
SETUP_AT = (5, 7, 9)
GATHERS = (0, 1, 2, 6, 7, 3, 4, 5)
EARLY = (6, 7)
STORES = (0, 1, 2, 3, 4, 6, 5, 7)
CHAIN = 7


def block_kernel(nc, x, W_in, conv_w, conv_b, W_x, W_dt, b_dt, A_log, D_skip, W_out,
                 w_gate, w1, w3, w2, out):
    xs_dram = nc.dram_tensor("moe_in", (EXPERTS * REGION, ROW), F32, kind="Internal").ap()
    ys_dram = nc.dram_tensor("moe_out", (MOE_TILES * SLOTS, D), F32, kind="Internal").ap()

    ctx = ExitStack()
    with ctx:
        def sb(name, shape, dt=F32):
            return ctx.enter_context(nc.sbuf_tensor(name, shape, dt))

        def pb(name):
            return ctx.enter_context(nc.psum_tensor(name, [P, 2 * GROUP], F32))

        def sem(name):
            return ctx.enter_context(nc.semaphore(name))

        xacc = sb("xacc", [P, TILES, D])
        xnT = sb("xnT", [P, TOKENS])
        xn = sb("xn", [P, TILES * ROW])
        xn_row = xn[:, :].rearrange("p (t r) -> p t r", r=ROW)
        WinT = sb("WinT", [P, 2 * INNER])
        Wc = sb("Wc", [P, HALVES, INNER])
        WgB = sb("WgB", [P, 4, P])
        WoT = sb("WoT", [P, HALVES, D])
        cw = sb("cw", [P, HALVES, TAPS])
        cb = sb("cb", [P, HALVES])
        bdt = sb("bdt", [P, HALVES])
        dsk = sb("dsk", [P, HALVES])
        dsk8 = sb("dsk8", [P, HALVES])
        wg = sb("wg", [P, EXPERTS])
        ident = sb("ident", [P, P])
        slot_u = sb("slot_u", [P, TOP_K, TILES], U32)
        eid_i = sb("eid_i", [P, MOE_TILES], I32)
        src_i = sb("src_i", [P, MOE_TILES], I32)
        back_u = sb("back_u", [P, TOP_K, TILES], U32)
        pad_i = sb("pad_i", [P, EXPERTS], I32)
        nbdt = sb("nbdt", [P, HALVES])
        bdt05 = sb("bdt05", [P, HALVES])
        chosen = sb("chosen", [P, TOP_K, TILES, EXPERTS])
        sf = sb("sf", [P, TOP_K, TILES])
        move_row = sb("move_row", [P, EXPERTS])
        zrow = sb("zrow", [P, 1, ROW])
        tile_oh = sb("tile_oh", [P, MOE_TILES, EXPERTS])
        slot_pe = sb("slot_pe", [P, GT, EXPERTS])
        slot_p = sb("slot_p", [P, 2, GT])

        acc = sb("acc", [P, HALVES, GROUP])
        xc = sb("xc", [P, SLOT3, HALVES, GROUP])
        sz = sb("sz", [P, SLOT3, HALVES, GROUP])
        ebuf = sb("ebuf", [P, HALVES, GROUP])
        th = sb("th", [P, HALVES, GROUP])
        al = sb("al", [P, HALVES, GROUP])
        gbuf = sb("gbuf", [P, HALVES, GROUP])
        hbuf = sb("hbuf", [P, HALVES, GROUP])
        ybuf = sb("ybuf", [P, HALVES, GROUP])
        y2 = sb("y2", [P, HALVES, GROUP])
        thg = sb("thg", [P, SLOT3, 2, GROUP])

        whi = sb("whi", [P, 2, 2 * HID], F32R)
        wlo = sb("wlo", [P, 2, 2 * HID], F32R)
        xhi = sb("xhi", [P, 2, SLOTS], F32R)
        xlo = sb("xlo", [P, 2, SLOTS], F32R)

        def in_xn(at, n):
            return xn[:, at:at + n]
        w13 = [in_xn(512 * b, 512) for b in range(2)]
        w2b = [in_xn(1024 + 256 * b, 256) for b in range(2)]
        xs = [in_xn(1536 + GT * ROW * b, GT * ROW).rearrange("p (j r) -> p j r", j=GT) for b in range(2)]
        sil = in_xn(2624, 1024)
        hid = [in_xn(3648 + 1024 * b, 1024) for b in range(2)]
        yo = [in_xn(5696 + 512 * b, 512) for b in range(2)]

        def flat(t):
            return t.rearrange("p a b -> p (a b)")
        win_raw = flat(acc[:, :, :])[:, 0:512].rearrange("p (a b) -> p a b", a=4)
        wdt_raw = flat(acc[:, :, :])[:, 512:1024].rearrange("p (a b) -> p a b", a=2)
        wx_raw = flat(ebuf[:, :, :])[:, 0:512].rearrange("p (a b) -> p a b", a=2)
        wxB = ebuf[0:STATE, 1, 0:256]
        wxC = ebuf[0:STATE, 1, 256:512]
        wo_raw = flat(th[:, :, :])[:, 0:256]
        wdtT = flat(th[:, :, :])[:, 512:1024].rearrange("p (a b) -> p a b", a=2)
        inv16 = th[0:STATE, 0, 256:256 + P]
        ones_pp = flat(al[:, :, :])[:, 0:128]
        tri = flat(al[:, :, :])[:, 128:256]
        iot = flat(al[:, :, :])[:, 256:640].bitcast(I32)
        ones64 = flat(al[:, :, :])[:, 640:704]
        thr = flat(al[:, :, :])[:, 704:832].rearrange("p (e m) -> p e m", e=EXPERTS)
        rev = flat(al[:, :, :])[:, 832:840]
        tix = flat(al[:, :, :])[:, 840:840 + MOE_TILES]
        nte = flat(al[:, :, :])[:, 896:904]
        nti = flat(al[:, :, :])[:, 904:912]
        reg0 = flat(al[:, :, :])[:, 912:920]
        eid_f = flat(al[:, :, :])[:, 920:920 + MOE_TILES]
        row_f = flat(al[:, :, :])[:, 960:960 + MOE_TILES]
        skip = flat(al[:, :, :])[:, 1000:1008]
        pad_f = flat(al[:, :, :])[:, 1008:1016]
        st = flat(gbuf[:, :, :])[:, 0:QT * 6].rearrange("p (j s) -> p j s", s=6)
        mv = flat(gbuf[:, :, :])[:, 128:128 + QT * 2].rearrange("p (j s) -> p j s", s=2)
        var = flat(gbuf[:, :, :])[:, 192:192 + QT]
        std = flat(gbuf[:, :, :])[:, 224:224 + QT]
        rst = flat(gbuf[:, :, :])[:, 256:256 + QT]
        nrt = flat(gbuf[:, :, :])[:, 288:288 + QT]

        def je(t):
            return t.rearrange("p (j e) -> p j e", e=EXPERTS)
        L = je(hbuf[:, 0, :])
        L2 = je(hbuf[:, 1, :])
        oh1, oh2 = chosen[:, 0], chosen[:, 1]
        msk = je(y2[:, 0, :])
        tmp = je(y2[:, 1, :])
        tot = je(sz[:, 2, 0, :])
        inc = je(sz[:, 2, 1, :])
        m1 = gbuf[:, 1, 0:64]
        m2 = gbuf[:, 1, 64:128]
        c1 = gbuf[:, 1, 128:192]
        dlt = gbuf[:, 1, 320:384]
        den = gbuf[:, 1, 384:448]
        prob = flat(xc[:, 2, :, :])[:, 936:936 + 64]
        cmp_m = flat(xc[:, 2, :, :])[:, 0:EXPERTS * 16].rearrange("p (e m) -> p e m", e=EXPERTS)
        cmp_t = flat(xc[:, 2, :, :])[:, 128:128 + MOE_TILES * EXPERTS].rearrange("p (t e) -> p t e", e=EXPERTS)
        cmp_s = flat(xc[:, 2, :, :])[:, 512:512 + MOE_TILES * EXPERTS].rearrange("p (t e) -> p t e", e=EXPERTS)
        tail = flat(xc[:, 2, :, :])[:, 896:896 + MOE_TILES]

        PA, PB, PC, PD = pb("PA"), pb("PB"), pb("PC"), pb("PD")

        s_x = [sem(f"s_x_{q}") for q in range(QUARTERS)]
        s_x0 = sem("s_x0")
        s_wg = sem("s_wg")
        s_wld = sem("s_wld")
        s_zrow = sem("s_zrow")
        s_fill = sem("s_fill")
        s_cst = sem("s_cst")
        s_wtp = sem("s_wtp")
        s_wcp = sem("s_wcp")
        s_dve = sem("s_dve")
        s_var = sem("s_var")
        s_std = sem("s_std")
        s_xn = sem("s_xn")
        s_xt = sem("s_xt")
        s_xnT = sem("s_xnT")
        s_lg = sem("s_lg")
        s_lcp = sem("s_lcp")
        s_msk = sem("s_msk")
        s_rk = sem("s_rk")
        s_dlt = sem("s_dlt")
        s_edl = sem("s_edl")
        s_slot = sem("s_slot")
        s_eid = sem("s_eid")
        s_tab = sem("s_tab")
        s_back = sem("s_back")
        s_scat = sem("s_scat")
        s_xp = sem("s_xp")
        s_z = sem("s_z")
        s_tap0 = sem("s_tap0")
        s_taps = sem("s_taps")
        s_cv = sem("s_cv")
        s_xc = sem("s_xc")
        s_sz = sem("s_sz")
        s_u = sem("s_u")
        s_g = sem("s_g")
        s_abs = sem("s_abs")
        s_exp = sem("s_exp")
        s_ln = sem("s_ln")
        s_dt = sem("s_dt")
        s_th = sem("s_th")
        s_al = sem("s_al")
        s_thg = sem("s_thg")
        s_ch = sem("s_ch")
        s_y2 = sem("s_y2")
        s_out = sem("s_out")
        s_add = sem("s_add")
        s_w13 = [sem(f"s_w13_{b}") for b in range(2)]
        s_w2 = [sem(f"s_w2_{b}") for b in range(2)]
        s_xs = [sem(f"s_xs_{b}") for b in range(2)]
        s_ys = [sem(f"s_ys_{b}") for b in range(2)]
        s_whi = sem("s_whi")
        s_wlo = sem("s_wlo")
        s_T = sem("s_T")
        s_xhi = sem("s_xhi")
        s_xlo = sem("s_xlo")
        s_h1 = sem("s_h1")
        s_h3 = sem("s_h3")
        s_sil = sem("s_sil")
        s_hid = sem("s_hid")
        s_y = sem("s_y")
        s_yc = sem("s_yc")
        s_pe = sem("s_pe")
        s_ps = sem("s_ps")
        s_got = [sem(f"s_got_{k}") for k in range(GROUPS // 2)]
        s_store = sem("s_store")

        x_q = x.rearrange("b l d -> (b l) d").rearrange("(q j p) d -> q p j d", q=QUARTERS, p=P)
        out_t = out.rearrange("b l d -> (b l) d").rearrange("(j p) d -> p j d", p=P)

        ys_tile = ys_dram.rearrange("(t j p) d -> p t j d", p=P, j=GT)

        ctx.enter_context(nc.allow_non_contiguous_dma(reason="three vectors of 256 elements"))
        block = ctx.enter_context(nc.Block())

        def mixer(eng, step, first, last):
            def whole(g):
                step(g, g % SLOT3, g + 1 < GROUPS, 0 <= g < GROUPS, 1 <= g <= GROUPS, g >= 2)
            start = max(first, 2)
            for g in range(first, min(start, last)):
                whole(g)
            turns = max(min(last, GROUPS - 1) - start, 0) // SLOT3
            if turns:
                with eng.Fori(0, turns) as i:
                    for k in range(SLOT3):
                        step(i * SLOT3 + (start + k), (start + k) % SLOT3, True, True, True, True)
            for g in range(start + turns * SLOT3, last):
                whole(g)

        @block.sync
        def _(sp):
            for q in range(QUARTERS):
                if q == 0:
                    sp.dma_start(xacc[:, 0:QT // 2, :], x_q[q][:, 0:QT // 2]).then_inc(s_x0, 16)
                    sp.dma_start(xacc[:, QT // 2:QT, :], x_q[q][:, QT // 2:QT]).then_inc(s_x[q], 16)
                else:
                    sp.dma_start(xacc[:, q * QT:(q + 1) * QT, :], x_q[q]).then_inc(s_x[q], 16)
                if q == 0:
                    sp.dma_start(wg[:, :], w_gate).then_inc(s_wg, 16)
            sp.dma_start(win_raw, W_in.rearrange("(a p) h -> p a h", p=P)).then_inc(s_wld, 16)
            sp.dma_start(wdt_raw, W_dt.rearrange("(a p) k -> p a k", p=P)).then_inc(s_wld, 16)
            sp.dma_start(wx_raw, W_x[2 * STATE:, :].rearrange("(a p) i -> p a i", p=P)).then_inc(s_wld, 16)
            sp.dma_start(wxB, W_x[0:STATE, :]).then_inc(s_wld, 16)
            sp.dma_start(wxC, W_x[STATE:2 * STATE, :]).then_inc(s_wld, 16)
            sp.dma_start(wo_raw, W_out).then_inc(s_wld, 16)
            sp.dma_start(cw[:, :, :], conv_w.rearrange("(c p) o k -> p c (o k)", p=P)).then_inc(s_wld, 16)
            sp.dma_start(cb[:, :], conv_b.rearrange("(c p) -> p c", p=P)).then_inc(s_wld, 16)
            sp.dma_start(bdt[:, :], b_dt.rearrange("(c p) -> p c", p=P)).then_inc(s_wld, 16)
            sp.dma_start(dsk[:, :], D_skip.rearrange("(c p) -> p c", p=P)).then_inc(s_wld, 16)
            def entry(table, t, last):
                at = slice(t, t + 1) if isinstance(t, int) else bass.ds(t, 1)
                return sp.value_load(table[0:1, at], min_val=0, max_val=last)

            def load_up(t, b, first):
                e = entry(eid_i, t, EXPERTS - 1)
                row = entry(src_i, t, EXPERTS * REGION - SLOTS)
                if not first:
                    sp.wait_ge(s_whi, t - 1)
                    sp.wait_ge(s_wlo, t - 1)
                dst = w13[b].rearrange("p (a h) -> p a h", a=2)
                sp.dma_start(dst[:, 0, :], w1[bass.ds(e, 1)].rearrange("e d h -> d (e h)")).then_inc(s_w13[b], 16)
                sp.dma_start(dst[:, 1, :], w3[bass.ds(e, 1)].rearrange("e d h -> d (e h)")).then_inc(s_w13[b], 16)
                if not first:
                    sp.wait_ge(s_T, t - 1)
                    sp.wait_ge(s_pe, t - 1)
                sp.dma_start(xs[b],
                             xs_dram[bass.ds(row, SLOTS), :].rearrange("(j p) d -> p j d", p=P)).then_inc(s_xs[b], 16)

            def load_down(t, b, first):
                e = entry(eid_i, t, EXPERTS - 1)
                if not first:
                    sp.wait_ge(s_y, t - 1)
                sp.dma_start(w2b[b].rearrange("p (o k d) -> p o k d", o=1, k=HALVES),
                             w2[bass.ds(e, 1)].rearrange("e (k p) d -> p e k d", p=P)).then_inc(s_w2[b], 16)

            def store(t, b):
                sp.wait_ge(s_yc, t + 1)
                dst = ys_tile[:, t:t + 1] if isinstance(t, int) else ys_tile[:, bass.ds(t, 1)]
                sp.dma_start(dst, yo[b].rearrange("p (o j d) -> p o j d", o=1, j=GT)).then_inc(s_ys[b], 16)

            sp.wait_ge(s_eid, 1)
            sp.wait_ge(s_zrow, 1)
            for e in range(EXPERTS):
                row = entry(pad_i, e, EXPERTS * REGION - SLOTS)
                sp.dma_start(xs_dram[bass.ds(row, SLOTS), :].rearrange("(j p) d -> p j d", p=P),
                             zrow[:, :, :].broadcast_to([P, GT, ROW])).then_inc(s_fill, 16)
            sp.wait_ge(s_fill, 16 * EXPERTS)
            sp.wait_ge(s_scat, 16 * TOP_K * TILES)
            load_up(0, 0, True)
            load_down(0, 0, True)
            load_up(1, 1, True)
            load_down(1, 1, True)
            load_up(2, 0, False)
            load_up(3, 1, False)
            with sp.Fori(0, (MOE_TILES - 5) // 2) as i:
                load_down(i * 2 + 2, 0, False)
                store(i * 2, 0)
                load_up(i * 2 + 4, 0, False)
                load_down(i * 2 + 3, 1, False)
                store(i * 2 + 1, 1)
                load_up(i * 2 + 5, 1, False)
            t = MOE_TILES - 3
            load_down(t, 0, False)
            store(t - 2, 0)
            load_up(t + 2, 0, False)
            load_down(t + 1, 1, False)
            store(t - 1, 1)
            load_down(t + 2, 0, False)
            for t in range(MOE_TILES - 3, MOE_TILES):
                store(t, t % 2)

            for k in STORES:
                sp.wait_ge(s_add, 2 * k + 3)
                sp.wait_ge(s_got[k], FILLED * TOP_K)
                at = slice(2 * k * GT, (2 * k + 2) * GT)
                sp.dma_start(out_t[:, at], xacc[:, at]).then_inc(s_store, 16)
            sp.wait_ge(s_store, 16 * (GROUPS // 2))

        @block.gpsimd
        def _(gp):
            gp.memset(ident[:, :], 0.0).then_inc(s_cst, 1)
            gp.memset(tri, 0.0).then_inc(s_cst, 1)
            gp.memset(ones_pp, 1.0).then_inc(s_cst, 1)
            gp.memset(inv16, 1.0 / STATE).then_inc(s_cst, 1)
            gp.memset(ones64, 1.0).then_inc(s_cst, 1)
            gp.iota(iot[:, 0:128], [[0, EXPERTS], [SLOTS, 16]], base=0, channel_multiplier=0).then_inc(s_cst, 1)
            gp.iota(iot[:, 128:128 + EXPERTS], [[-1, EXPERTS]], base=EXPERTS, channel_multiplier=0).then_inc(s_cst, 1)
            gp.iota(iot[:, 256:256 + MOE_TILES], [[1, MOE_TILES]], base=0, channel_multiplier=0).then_inc(s_cst, 1)
            gp.iota(iot[:, 320:320 + EXPERTS], [[REGION, EXPERTS]], base=0, channel_multiplier=0).then_inc(s_cst, 1)
            gp.wait_ge(s_cst, 9)
            gp.affine_select(out=ident[:, :], in_=ident[:, :], compare_op=ALU.not_equal, fill=1.0,
                             base=0, pattern=[[-1, P]], channel_multiplier=1).then_inc(s_cst, 1)
            gp.affine_select(out=tri, in_=tri, compare_op=ALU.is_ge, fill=1.0,
                             base=0, pattern=[[-1, P]], channel_multiplier=1).then_inc(s_cst, 1)
            for n, (q0, qn) in enumerate(CHUNKS):
                gp.wait_ge(s_slot, n + 1)
                for j in range(q0 * QT, (q0 + qn) * QT):
                    for k in range(TOP_K):
                        gp.indirect_dma_start(xs_dram, bass.IndirectOffsetOnAxis(ap=slot_u[:, k, j:j + 1], axis=0),
                                              xn_row[:, j, :], None).then_inc(s_scat, 16)

            def step(t, n, b, more):
                gp.wait_ge(s_whi, t + 1)
                if not (isinstance(t, int) and t < 2):
                    gp.wait_ge(s_h3, t - 1)
                gp.tensor_tensor(wlo[:, b, :], w13[b], whi[:, b, :].bitcast(F32), ALU.subtract).then_inc(s_wlo, 1)
            step(0, 0, 0, True)
            step(1, 0, 1, True)
            with gp.Fori(0, (MOE_TILES - 3) // 2) as i:
                step(i * 2 + 2, i + 1, 0, True)
                step(i * 2 + 3, i + 1, 1, True)
            step(MOE_TILES - 1, 0, 0, False)

            gp.wait_ge(s_back, TOP_K)
            gp.wait_ge(s_ys[0], 16 * ((MOE_TILES + 1) // 2))
            gp.wait_ge(s_ys[1], 16 * (MOE_TILES // 2))
            def gather(k, c):
                if c:
                    gp.wait_ge(s_got[k], FILLED)
                elif k not in EARLY:
                    gp.wait_ge(s_add, 2 * k + 3)
                for tile in range(2 * k * GT, 2 * (k + 1) * GT):
                    gp.indirect_dma_start(
                        xacc[:, tile, :], None, ys_dram,
                        bass.IndirectOffsetOnAxis(ap=back_u[:, c, tile:tile + 1], axis=0),
                        compute_op=ALU.add).then_inc(s_got[k], 16)

            for n, k in enumerate(GATHERS):
                gather(k, 0)
                if n:
                    gather(GATHERS[n - 1], 1)
            gather(GATHERS[-1], 1)

        @block.tensor
        def _(pe):
            def setup(r):
                if r == 0:
                    pe.wait_ge(s_wld, 16 * 10)
                    for a in range(4):
                        pe.transpose(PB[:, a * P:(a + 1) * P], win_raw[:, a, :], ident[:, :])
                    for kb in range(2):
                        for ob in range(2):
                            at = 512 + kb * 256 + ob * 128
                            last = pe.transpose(PB[:, at:at + P], wdt_raw[:, ob, kb * P:(kb + 1) * P], ident[:, :])
                elif r == 1:
                    pe.wait_ge(s_wcp, 2)
                    for ib in range(2):
                        pe.transpose(PB[:, ib * P:(ib + 1) * P], wo_raw[:, ib * P:(ib + 1) * P], ident[:, :])
                    for n, rows in enumerate((wxB, wxC)):
                        for ib in range(2):
                            at = 512 + (n * 2 + ib) * P
                            last = pe.matmul(PB[:, at:at + P], rows[:, ib * P:(ib + 1) * P], inv16, start=True, stop=True)
                else:
                    pe.wait_ge(s_wcp, 4)
                    for ib in range(2):
                        for kb in range(2):
                            last = pe.matmul(PB[:, ib * 256:(ib + 1) * 256], wx_raw[:, kb, ib * P:(ib + 1) * P],
                                             wdtT[:, kb, :], start=(kb == 0), stop=(kb == 1))
                last.then_inc(s_wtp, 1)

            pe.wait_ge(s_cst, 11)
            pe.wait_ge(s_wg, 16)
            def logits(g):
                pe.wait_ge(s_xnT, g + 1)
                q = g * GT // QT
                if q >= 2:
                    pe.wait_ge(s_lcp, q - 1)
                for j in range(GT * g, GT * g + GT):
                    at = (q + 1) % 2 * 512 + j * EXPERTS
                    last = pe.matmul(PC[:, at:at + EXPERTS], xnT[:, j * P:(j + 1) * P],
                                     wg[:, :], start=True, stop=True)
                last.then_inc(s_lg, 1)

            def ranks(n):
                q0, qn = CHUNKS[n]
                pe.wait_ge(s_msk, n + 1)
                m = msk[:, q0 * QT:(q0 + qn) * QT, :].rearrange("p j e -> p (j e)")
                at, to = q0 * QT * EXPERTS, (q0 + qn) * QT * EXPERTS
                pe.matmul(PD[:, at:to], tri, m, start=True, stop=True).then_inc(s_rk, 1)
                pe.matmul(PD[:, 512 + at:512 + to], ones_pp, m, start=True, stop=True).then_inc(s_rk, 1)

            def mix(g, slot, a, b, c, d):
                static = isinstance(g, int)
                if a:
                    src = xnT[:, bass.ds(g * GROUP + GROUP, GROUP)] if not static else \
                        xnT[:, (g + 1) * GROUP:(g + 2) * GROUP]
                    if not (static and g + 1 < 1):
                        pe.wait_ge(s_taps, g + 1)
                    for c_ in range(HALVES):
                        last = pe.matmul(PA[:, c_ * GROUP:(c_ + 1) * GROUP], WinT[:, c_ * P:(c_ + 1) * P], src,
                                         start=True, stop=True)
                    last.then_inc(s_xp, 1)
                if d:
                    pe.wait_ge(s_y2, g - 1)
                    if b:
                        pe.wait_ge(s_sz, g + 1)
                    else:
                        pe.wait_ge(s_add, g - 1)
                    for j in range(GT):
                        for k in range(HALVES):
                            last = pe.matmul(PB[:, j * D:(j + 1) * D], y2[:, k, j * P:(j + 1) * P], WoT[:, k, :],
                                             start=(k == 0), stop=(k == 1))
                    last.then_inc(s_out, 1)
                if b:
                    pe.wait_ge(s_xc, g + 1)
                    if not (static and g < 1):
                        pe.wait_ge(s_dt, g)
                    else:
                        pe.wait_ge(s_lcp, QUARTERS)
                    for c_ in range(HALVES):
                        for k in range(HALVES):
                            last = pe.matmul(PC[:, c_ * GROUP:(c_ + 1) * GROUP], Wc[:, k, c_ * P:(c_ + 1) * P],
                                             xc[:, slot, k, :], start=(k == 0), stop=(k == 1))
                    last.then_inc(s_u, 1)
                if a:
                    if not (static and g + 1 < 1):
                        pe.wait_ge(s_sz, g + 1)
                    if d:
                        pe.wait_ge(s_add, g)
                    for c_ in range(HALVES):
                        last = pe.matmul(PB[:, c_ * GROUP:(c_ + 1) * GROUP],
                                         WinT[:, INNER + c_ * P:INNER + (c_ + 1) * P], src, start=True, stop=True)
                    last.then_inc(s_z, 1)
                if b:
                    if not (static and g < 1):
                        pe.wait_ge(s_thg, g)
                    else:
                        pe.wait_ge(s_slot, len(CHUNKS))
                    for n in range(2):
                        for k in range(HALVES):
                            last = pe.matmul(PD[:, n * GROUP:(n + 1) * GROUP], WgB[:, n * 2 + k, :],
                                             xc[:, slot, k, :], start=(k == 0), stop=(k == 1))
                    last.then_inc(s_g, 1)

            for g in range(GROUPS):
                pe.wait_ge(s_xn, g + 1)
                if g >= 2:
                    pe.wait_ge(s_xnT, g - 1)
                for j in range(GT):
                    t = g * GT + j
                    at = (g % 2) * 512 + j * P
                    last = pe.transpose(PA[:, at:at + P], xn_row[:, t, 0:D], ident[:, :])
                last.then_inc(s_xt, 1)
                if g * GT % QT:
                    logits(g - 1)
                if (g + 1) * GT % QT == 0:
                    logits(g)
                if g in SETUP_AT:
                    setup(SETUP_AT.index(g))
                for n, (q0, qn) in enumerate(CHUNKS):
                    if g == min(q0 + qn + 1, QUARTERS) * QT // GT - 1:
                        if n == len(CHUNKS) - 1:
                            pe.wait_ge(s_xnT, GROUPS)
                            pe.wait_ge(s_wcp, 8)
                            mixer(pe, mix, -1, 0)
                        ranks(n)

            pe.sem_inc(s_out, 1)
            mixer(pe, mix, 0, STEPS_A)

            def transp(t, n, b, first):
                pe.wait_ge(s_xs[b], n * 16 + 16)
                if not first:
                    pe.wait_ge(s_xhi, t)
                    pe.wait_ge(s_xlo, t)
                for j in range(GT):
                    last = pe.transpose(PD[:, j * P:(j + 1) * P], xs[b][:, j, 0:D], ident[:, :])
                last.then_inc(s_T, 1)

            def up(t, b, first):
                pe.wait_ge(s_wlo, t + 1)
                pe.wait_ge(s_xhi, t + 1)
                for m, (ps, free, done) in enumerate(((PA, s_sil, s_h1), (PB, s_hid, s_h3))):
                    if not first:
                        pe.wait_ge(free, t)
                    out_c = [ps[:, c_ * SLOTS:(c_ + 1) * SLOTS] for c_ in range(HALVES)]
                    w_c = [slice(m * HID + c_ * P, m * HID + (c_ + 1) * P) for c_ in range(HALVES)]
                    for o, at in zip(out_c, w_c):
                        pe.matmul(o, whi[:, b, at], xhi[:, b, :], start=True, stop=False)
                        pe.matmul(o, wlo[:, b, at], xhi[:, b, :], start=False, stop=False)
                    pe.wait_ge(s_xlo, t + 1)
                    for o, at in zip(out_c, w_c):
                        last = pe.matmul(o, whi[:, b, at], xlo[:, b, :], start=False, stop=True)
                    last.then_inc(done, 1)

            def down(t, n, b, first):
                pe.wait_ge(s_hid, t + 1)
                pe.wait_ge(s_w2[b], n * 16 + 16)
                if not first:
                    pe.wait_ge(s_yc, t)
                for j in range(GT):
                    for k in range(HALVES):
                        last = pe.matmul(PD[:, 512 + j * D:512 + (j + 1) * D],
                                         hid[b][:, k * SLOTS + j * P:k * SLOTS + (j + 1) * P],
                                         w2b[b][:, k * D:(k + 1) * D], start=(k == 0), stop=(k == 1))
                last.then_inc(s_y, 1)

            pe.wait_ge(s_thg, STEPS_A)
            pe.wait_ge(s_taps, STEPS_A + 1)
            pe.wait_ge(s_sz, STEPS_A + 1)
            pe.wait_ge(s_add, STEPS_A - 1)
            transp(0, 0, 0, True)
            up(0, 0, True)
            transp(1, 0, 1, False)
            up(1, 1, False)
            transp(2, 1, 0, False)
            down(0, 0, 0, True)
            with pe.Fori(0, (MOE_TILES - 3) // 2) as i:
                up(i * 2 + 2, 0, False)
                transp(i * 2 + 3, i + 1, 1, False)
                down(i * 2 + 1, i, 1, False)
                up(i * 2 + 3, 1, False)
                transp(i * 2 + 4, i + 2, 0, False)
                down(i * 2 + 2, i + 1, 0, False)
            t = MOE_TILES - 1
            up(t, 0, False)
            down(t - 1, (t - 1) // 2, 1, False)
            down(t, t // 2, 0, False)

            pe.wait_ge(s_sil, MOE_TILES)
            pe.wait_ge(s_hid, MOE_TILES)
            pe.wait_ge(s_yc, MOE_TILES)
            mixer(pe, mix, STEPS_A, GROUPS + 2)

        @block.scalar
        def _(act):
            act.preload_act_table_set("sqrt_and_others")
            def setup(r):
                act.wait_ge(s_wtp, r + 1)
                if r == 0:
                    act.activation(WinT[:, :], PB[:, 0:512], ACT.Copy).then_inc(s_wcp, 1)
                    act.activation(wdtT, PB[:, 512:1024].rearrange("p (a b) -> p a b", a=2), ACT.Copy).then_inc(s_wcp, 1)
                elif r == 1:
                    act.activation(WoT[:, :, :], PB[:, 0:256].rearrange("p (a b) -> p a b", a=2), ACT.Copy,
                                   scale=-0.125).then_inc(s_wcp, 1)
                    act.activation(WgB[:, :, :], PB[:, 512:1024].rearrange("p (a b) -> p a b", a=4),
                                   ACT.Copy).then_inc(s_wcp, 1)
                else:
                    act.activation(Wc[:, :, :], PB[:, 0:512].rearrange("p (a b) -> p a b", a=2),
                                   ACT.Copy).then_inc(s_wcp, 1)
                    act.activation(dsk8[:, :], dsk[:, :], ACT.Copy, scale=-8.0).then_inc(s_wcp, 1)
                    act.activation(nbdt[:, :], bdt[:, :], ACT.Copy, scale=-1.0).then_inc(s_wcp, 1)
                    act.activation(bdt05[:, :], bdt[:, :], ACT.Copy, scale=0.05).then_inc(s_wcp, 1)

            def softmax_exp(n):
                q0, qn = CHUNKS[n]
                J = slice(q0 * QT, (q0 + qn) * QT)
                act.preload_act_table_set("natural_log_exp_and_others")
                act.wait_ge(s_dlt, n + 1)
                act.activation(den[:, J], dlt[:, J], ACT.Exp).then_inc(s_edl, 1)

            for q in range(QUARTERS):
                act.wait_ge(s_var, q + 1)
                act.activation(std, var, ACT.Sqrt).then_inc(s_std, 1)
                if q == 2:
                    softmax_exp(0)
                    act.preload_act_table_set("sqrt_and_others")
                for g in range(q * GROUPS // QUARTERS, (q + 1) * GROUPS // QUARTERS):
                    act.wait_ge(s_xt, g + 1)
                    act.activation(xnT[:, g * GROUP:(g + 1) * GROUP], PA[:, (g % 2) * 512:(g % 2) * 512 + 512],
                                   ACT.Copy).then_inc(s_xnT, 1)
                    if g - 1 in SETUP_AT:
                        setup(SETUP_AT.index(g - 1))
            def mix(g, slot, a, b, c, d):
                static = isinstance(g, int)
                nxt = (slot + 1) % SLOT3
                if not (b or c):
                    act.preload_act_table_set("silu_and_others")
                if a:
                    act.wait_ge(s_xp, g + 2)
                    if not (static and g + 1 < 1):
                        act.wait_ge(s_xc, g + 1)
                    for c_ in range(HALVES):
                        last = act.activation(acc[:, c_, :], PA[:, c_ * GROUP:(c_ + 1) * GROUP], ACT.Identity,
                                              bias=cb[:, c_:c_ + 1], scale=cw[:, c_, TAPS - 1:TAPS])
                    last.then_inc(s_tap0, 1)
                if c:
                    act.wait_ge(s_dt, g)
                    if not (static and g < 2):
                        act.wait_ge(s_ch, g * CHAIN - 2 * CHAIN + 1)
                    for c_ in range(HALVES):
                        last = act.activation(th[:, c_, :], ebuf[:, c_, :], ACT.Tanh, scale=0.05,
                                              bias=bdt05[:, c_:c_ + 1])
                    last.then_inc(s_th, 1)
                    act.wait_ge(s_th, g)
                    if not (static and g < 2):
                        act.wait_ge(s_ch, g * CHAIN - 2 * CHAIN + 5)
                    act.activation(al[:, :, :], th[:, :, :], ACT.Copy, bias=0.5, scale=0.5).then_inc(s_al, 1)
                if b:
                    act.preload_act_table_set("natural_log_exp_and_others")
                    act.wait_ge(s_u, g + 1)
                    if not (static and g < 1):
                        act.wait_ge(s_th, g)
                    for c_ in range(HALVES):
                        last = act.activation(ebuf[:, c_, :], PC[:, c_ * GROUP:(c_ + 1) * GROUP], ACT.Abs,
                                              bias=bdt[:, c_:c_ + 1])
                    last.then_inc(s_abs, 1)
                    act.wait_ge(s_abs, g + 1)
                    act.activation(ebuf[:, :, :], ebuf[:, :, :], ACT.Exp, scale=-1.0).then_inc(s_exp, 1)
                    act.wait_ge(s_exp, g + 1)
                    act.activation(ebuf[:, :, :], ebuf[:, :, :], ACT.Ln, bias=1.0).then_inc(s_ln, 1)
                    act.preload_act_table_set("silu_and_others")
                if a:
                    act.wait_ge(s_z, g + 2)
                    act.activation(sz[:, nxt].rearrange("p a b -> p (a b)"), PB[:, :], ACT.Silu).then_inc(s_sz, 1)
                if b:
                    act.wait_ge(s_g, g + 1)
                    act.activation(thg[:, slot].rearrange("p a b -> p (a b)"), PD[:, :], ACT.Tanh,
                                   scale=0.5).then_inc(s_thg, 1)
                if a:
                    act.wait_ge(s_taps, g + 2)
                    act.activation(xc[:, nxt], acc[:, :, :], ACT.Silu).then_inc(s_xc, 1)

            softmax_exp(1)
            mixer(act, mix, -1, 0)
            softmax_exp(2)
            mixer(act, mix, 0, 1)
            act.wait_ge(s_tab, 1)
            mixer(act, mix, 1, STEPS_A)

            def round_w(t, n, b, first):
                act.wait_ge(s_w13[b], n * 32 + 32)
                if not first:
                    act.wait_ge(s_h3, t - 1)
                act.activation(whi[:, b, :], w13[b], ACT.Copy).then_inc(s_whi, 1)

            def round_x(t, b):
                act.wait_ge(s_T, t + 1)
                act.activation(xhi[:, b, :], PD[:, 0:512], ACT.Copy).then_inc(s_xhi, 1)

            def gate(t, first):
                act.wait_ge(s_h1, t + 1)
                if not first:
                    act.wait_ge(s_hid, t)
                act.activation(sil, PA[:, :], ACT.Silu).then_inc(s_sil, 1)

            def tile_step(t, n, b, more):
                if more:
                    round_w(t + 1, n + b, 1 - b, False)
                gate(t, False)
                if more:
                    round_x(t + 1, 1 - b)

            round_w(0, 0, 0, True)
            round_x(0, 0)
            round_w(1, 0, 1, True)
            gate(0, True)
            round_x(1, 1)
            round_w(2, 1, 0, False)
            gate(1, False)
            round_x(2, 0)
            round_w(3, 1, 1, False)
            gate(2, False)
            round_x(3, 1)
            with act.Fori(0, (MOE_TILES - 5) // 2) as i:
                tile_step(i * 2 + 3, i + 1, 1, True)
                tile_step(i * 2 + 4, i + 2, 0, True)
            t = MOE_TILES - 2
            tile_step(t, t // 2, 1, True)
            tile_step(t + 1, (t + 1) // 2, 0, False)

            mixer(act, mix, STEPS_A, GROUPS + 2)

        @block.vector
        def _(ve):
            count = [0]

            def link(ins):
                count[0] += 1
                ins.then_inc(s_dve, 1)
                ve.wait_ge(s_dve, count[0])

            ve.memset(zrow[:, :, :], 0.0).then_inc(s_zrow, 1)
            ve.sem_inc(s_add, 1)

            def statistics(q):
                ve.wait_ge(s_x[q] if q else s_x0, 16)
                for j in range(QT):
                    if q == 0 and j == QT // 2:
                        ve.wait_ge(s_x[q], 16)
                    last = ve.bn_stats(st[:, j, :], xacc[:, q * QT + j, :])
                link(last)
                for j in range(QT):
                    last = ve.bn_aggr(mv[:, j, :], st[:, j, :])
                link(last)
                ve.tensor_scalar(var, mv[:, :, 1], EPS, None, ALU.add).then_inc(s_var, 1)
                ve.wait_ge(s_var, q + 1)
                ve.wait_ge(s_std, q + 1)
                link(ve.reciprocal(rst, std))
                link(ve.tensor_tensor(nrt, rst, rst, ALU.mult))
                link(ve.tensor_tensor(nrt, nrt, var, ALU.mult))
                link(ve.tensor_scalar(nrt, nrt, -0.5, 1.5, ALU.mult, ALU.add))
                link(ve.tensor_tensor(rst, rst, nrt, ALU.mult))

            def scale(q):
                for j in range(QT):
                    t = q * QT + j
                    last = ve.tensor_scalar(xn_row[:, t, 0:D], xacc[:, t, :], mv[:, j, 0:1], rst[:, j:j + 1],
                                            ALU.subtract, ALU.mult)
                    if j % GT == GT - 1:
                        last.then_inc(s_xn, 1)
                ve.wait_ge(s_xn, (q + 1) * QT // GT)

            def norm(q):
                statistics(q)
                scale(q)

            def pick(logit, best, oh, t_, c_, shape):
                rev_b = rev.unsqueeze(1).broadcast_to(shape)
                link(ve.reduce_max(best, logit, AX_X))
                link(ve.tensor_tensor(t_, logit, best.unsqueeze(2).broadcast_to(shape), ALU.is_equal))
                link(ve.tensor_tensor(t_, t_, rev_b, ALU.mult))
                link(ve.reduce_max(c_, t_, AX_X))
                link(ve.tensor_tensor(oh, rev_b, c_.unsqueeze(2).broadcast_to(shape), ALU.is_equal))

            def take_logits(q):
                ve.wait_ge(s_lg, (q + 1) * QT // GT)
                at, Q = (q + 1) % 2 * 512, slice(q * QT, (q + 1) * QT)
                ve.tensor_copy(L[:, Q, :], je(PC[:, at:at + 512])[:, Q, :]).then_inc(s_lcp, 1)

            def chunk(n):
                q0, qn = CHUNKS[n]
                return q0 * QT, qn * QT, slice(q0 * QT, (q0 + qn) * QT)

            def choose(n):
                j0, jn, J = chunk(n)
                shape = [P, jn, EXPERTS]
                ve.wait_ge(s_lcp, (j0 + jn) // QT)
                pick(L[:, J, :], m1[:, J], oh1[:, J, :], tmp[:, J, :], c1[:, J], shape)
                link(ve.scalar_tensor_tensor(L2[:, J, :], oh1[:, J, :], -3.0e38, L[:, J, :], ALU.mult, ALU.add))
                pick(L2[:, J, :], m2[:, J], oh2[:, J, :], tmp[:, J, :], c1[:, J], shape)
                ve.tensor_tensor(msk[:, J, :], oh1[:, J, :], oh2[:, J, :], ALU.add).then_inc(s_msk, 1)
                ve.tensor_tensor(dlt[:, J], m2[:, J], m1[:, J], ALU.subtract).then_inc(s_dlt, 1)

            def place(n):
                j0, jn, J = chunk(n)
                shape = [P, jn, EXPERTS]
                ve.wait_ge(s_rk, 2 * n + 2)
                link(ve.tensor_copy(tot[:, J, :], je(PD[:, 512:1024])[:, J, :]))
                for e in range(EXPERTS):
                    before = inc[:, j0 - 1, e:e + 1] if j0 else 0.0
                    last = ve.tensor_tensor_scan(inc[:, J, e], ones64[:, 0:jn], tot[:, J, e], before, ALU.mult, ALU.add)
                link(last)
                link(ve.tensor_tensor(tmp[:, J, :], inc[:, J, :], tot[:, J, :], ALU.subtract))
                link(ve.tensor_tensor(tmp[:, J, :], tmp[:, J, :], je(PD[:, 0:512])[:, J, :], ALU.add))
                link(ve.tensor_tensor(tmp[:, J, :], tmp[:, J, :], reg0.unsqueeze(1).broadcast_to(shape), ALU.add))
                for k, oh in enumerate((oh1, oh2)):
                    link(ve.tensor_tensor(L2[:, J, :], oh[:, J, :], tmp[:, J, :], ALU.mult))
                    link(ve.reduce_sum(sf[:, k, J], L2[:, J, :], AX_X))
                ve.wait_ge(s_edl, n + 1)
                link(ve.tensor_scalar(c1[:, J], den[:, J], 1.0, None, ALU.add))
                link(ve.reciprocal(prob[:, J], c1[:, J]))
                link(ve.tensor_tensor(c1[:, J], prob[:, J], den[:, J], ALU.mult))
                link(ve.tensor_tensor(L2[:, J, :], oh1[:, J, :], prob[:, J].unsqueeze(2).broadcast_to(shape), ALU.mult))
                link(ve.tensor_tensor(tmp[:, J, :], oh2[:, J, :], c1[:, J].unsqueeze(2).broadcast_to(shape), ALU.mult))
                link(ve.tensor_tensor(xn_row[:, J, D:ROW], L2[:, J, :], tmp[:, J, :], ALU.add))
                ve.tensor_copy(slot_u[:, :, J], sf[:, :, J]).then_inc(s_slot, 1)

            def chain(g, slot, part):
                prv = (slot + 2) % SLOT3
                gates = thg[:, prv]

                def step(ins):
                    ins.then_inc(s_ch, 1)

                def after(n):
                    ve.wait_ge(s_ch, g * CHAIN - CHAIN + n)
                if part == 0:
                    ve.wait_ge(s_th, g)
                    step(ve.scalar_tensor_tensor(gbuf[:, :, :], th[:, :, :], -1.0, xc[:, prv], ALU.add, ALU.mult))
                    ve.wait_ge(s_al, g)
                    step(ve.tensor_scalar(al[:, :, :], al[:, :, :], 0.01, 0.99, ALU.max, ALU.min))
                elif part == 1:
                    after(2)
                    step(ve.memset(al[:, :, :].rearrange("p a (s l) -> p a s l", s=SPG)[:, :, :, 0], 0.0))
                    ve.wait_ge(s_thg, g)
                    step(ve.scalar_tensor_tensor(gbuf[:, :, :], gates[:, 0:1, :].broadcast_to([P, HALVES, GROUP]), 1.0,
                                                 gbuf[:, :, :], ALU.add, ALU.mult))
                elif part == 2:
                    after(4)
                    step(ve.tensor_tensor_scan(hbuf[:, :, :].rearrange("p a b -> p (a b)"),
                                               al[:, :, :].rearrange("p a b -> p (a b)"),
                                               gbuf[:, :, :].rearrange("p a b -> p (a b)"), 0.0, ALU.mult, ALU.add))
                elif part == 3:
                    after(5)
                    step(ve.scalar_tensor_tensor(ybuf[:, :, :], gates[:, 1:2, :].broadcast_to([P, HALVES, GROUP]), 1.0,
                                                 hbuf[:, :, :], ALU.add, ALU.mult))
                else:
                    after(6)
                    for c_ in range(HALVES):
                        last = ve.scalar_tensor_tensor(ybuf[:, c_, :], xc[:, prv, c_, :], dsk8[:, c_:c_ + 1],
                                                       ybuf[:, c_, :], ALU.mult, ALU.add)
                    step(last)
                    after(7)
                    ve.wait_ge(s_out, g)
                    ve.tensor_tensor(y2[:, :, :], ybuf[:, :, :], sz[:, prv], ALU.mult).then_inc(s_y2, 1)

            def softplus(g):
                ve.wait_ge(s_ln, g + 1)
                for c_ in range(HALVES):
                    last = ve.scalar_tensor_tensor(ebuf[:, c_, :], PC[:, c_ * GROUP:(c_ + 1) * GROUP],
                                                   nbdt[:, c_:c_ + 1], ebuf[:, c_, :], ALU.max, ALU.add)
                last.then_inc(s_dt, 1)

            def tap(g, j, c_):
                if c_ == 0:
                    if j == 1:
                        ve.wait_ge(s_tap0, g + 2)
                    else:
                        ve.wait_ge(s_cv, g * 2 + j + 1)
                a_v = acc[:, c_, :].rearrange("p (s l) -> p s l", s=SPG)[:, :, j:SEQ]
                p_v = PA[:, c_ * GROUP:(c_ + 1) * GROUP].rearrange("p (s l) -> p s l", s=SPG)
                ins = ve.scalar_tensor_tensor(a_v, p_v[:, :, 0:SEQ - j], cw[:, c_, TAPS - 1 - j:TAPS - j],
                                              a_v, ALU.mult, ALU.add)
                if c_ == HALVES - 1:
                    ins.then_inc(s_taps if j == TAPS - 1 else s_cv, 1)

            def add_out(g):
                static = isinstance(g, int)
                ve.wait_ge(s_out, g)
                if static and (g - 2) // 2 in EARLY:
                    ve.wait_ge(s_got[(g - 2) // 2], FILLED * TOP_K)
                at = bass.ds(g * GT - 2 * GT, GT) if not static else slice((g - 2) * GT, (g - 1) * GT)
                ve.tensor_tensor(xacc[:, at, :], PB[:, 0:GROUP].rearrange("p (j d) -> p j d", j=GT),
                                 xacc[:, at, :], ALU.add).then_inc(s_add, 1)

            def mix(g, slot, a, b, c, d):
                if a:
                    tap(g, 1, 0)
                    tap(g, 1, 1)
                if d:
                    add_out(g)
                if c:
                    chain(g, slot, 0)
                if a:
                    tap(g, 2, 0)
                if c:
                    chain(g, slot, 1)
                if a:
                    tap(g, 2, 1)
                if c:
                    chain(g, slot, 2)
                if a:
                    tap(g, 3, 0)
                if c:
                    chain(g, slot, 3)
                if a:
                    tap(g, 3, 1)
                if c:
                    chain(g, slot, 4)
                if b:
                    softplus(g)

            def mix_before_experts(g, slot, a, b, c, d):
                tap(g, 1, 0)
                tap(g, 1, 1)
                add_out(g)
                chain(g, slot, 0)
                for j in (2, 3):
                    tap(g, j, 0)
                    tap(g, j, 1)
                softplus(g)

            norm(0)
            ve.wait_ge(s_cst, 11)
            ve.tensor_copy(thr, iot[:, 0:128].rearrange("p (e m) -> p e m", e=EXPERTS))
            ve.tensor_copy(rev, iot[:, 128:128 + EXPERTS])
            ve.tensor_copy(tix, iot[:, 256:256 + MOE_TILES])
            link(ve.tensor_copy(reg0, iot[:, 320:320 + EXPERTS]))
            norm(1)
            take_logits(0)
            choose(0)
            statistics(2)
            place(0)
            scale(2)
            take_logits(1)
            norm(3)
            take_logits(2)
            choose(1)
            place(1)
            take_logits(3)
            choose(2)
            mixer(ve, mix, -1, 0)
            place(2)

            cnt = inc[:, TILES - 1, :]
            link(ve.tensor_tensor(cmp_m, thr, cnt.unsqueeze(2).broadcast_to([P, EXPERTS, 16]), ALU.is_lt))
            link(ve.reduce_sum(nte, cmp_m, AX_X))
            link(ve.tensor_tensor_scan(nti, ones64[:, 0:EXPERTS], nte, 0.0, ALU.mult, ALU.add))
            te = [P, MOE_TILES, EXPERTS]
            link(ve.tensor_scalar(skip, nte, -float(SLOTS), float(REGION), ALU.mult, ALU.add))
            link(ve.tensor_tensor(cmp_t, nti.unsqueeze(1).broadcast_to(te), tix.unsqueeze(2).broadcast_to(te),
                                  ALU.is_le))
            link(ve.reduce_sum(eid_f, cmp_t, AX_X))
            link(ve.tensor_tensor(cmp_s, cmp_t, skip.unsqueeze(1).broadcast_to(te), ALU.mult))
            link(ve.reduce_sum(row_f, cmp_s, AX_X))
            link(ve.scalar_tensor_tensor(row_f, tix, float(SLOTS), row_f, ALU.mult, ALU.add))
            link(ve.tensor_scalar(tail, row_f, float(EXPERTS * REGION), None, ALU.is_lt))
            link(ve.tensor_tensor(row_f, row_f, tail, ALU.mult))
            link(ve.tensor_copy(src_i[:, :], row_f))
            link(ve.tensor_scalar(eid_f, eid_f, float(EXPERTS - 1), None, ALU.min))
            link(ve.tensor_tensor(pad_f, cnt, reg0, ALU.add))
            link(ve.tensor_copy(pad_i[:, :], pad_f))
            ve.tensor_copy(eid_i[:, :], eid_f).then_inc(s_eid, 1)
            link(ve.tensor_scalar(eid_f, eid_f, -1.0, float(EXPERTS), ALU.mult, ALU.add))
            link(ve.tensor_tensor(tile_oh[:, :, :], eid_f.unsqueeze(2).broadcast_to(te), rev.unsqueeze(1).broadcast_to(te),
                                  ALU.is_equal))
            move = move_row[:, :]
            link(ve.tensor_tensor(move, nti, nte, ALU.subtract))
            ve.scalar_tensor_tensor(move, move, float(SLOTS), reg0, ALU.mult, ALU.subtract).then_inc(s_tab, 1)
            mixer(ve, mix, 0, 1)
            ve.wait_ge(s_tab, 1)
            ve.wait_ge(s_slot, len(CHUNKS))
            ve.wait_ge(s_eid, 1)

            mixer(ve, mix, 1, STEPS_A - 1)
            mixer(ve, mix_before_experts, STEPS_A - 1, STEPS_A)

            def low(t, b, first):
                ve.wait_ge(s_xhi, t + 1)
                if not first:
                    ve.wait_ge(s_h3, t - 1)
                ve.tensor_tensor(xlo[:, b, :], PD[:, 0:512], xhi[:, b, :].bitcast(F32), ALU.subtract).then_inc(s_xlo, 1)

            def glu(t, b, first):
                ve.wait_ge(s_h3, t + 1)
                ve.wait_ge(s_sil, t + 1)
                if not first:
                    ve.wait_ge(s_y, t - 1)
                ve.tensor_tensor(hid[b], sil, PB[:, :], ALU.mult).then_inc(s_hid, 1)

            def own_p(t, n, b):
                ve.wait_ge(s_xs[b], n * 16 + 16)
                if not (isinstance(t, int) and t == 0):
                    ve.wait_ge(s_ps, t)
                at = slice(t, t + 1) if isinstance(t, int) else bass.ds(t, 1)
                ve.tensor_tensor(slot_pe[:, :, :], xs[b][:, :, D:ROW],
                                 tile_oh[:, at, :].broadcast_to([P, GT, EXPERTS]), ALU.mult).then_inc(s_pe, 1)

            def sum_p(t, b):
                ve.wait_ge(s_pe, t + 1)
                if not (isinstance(t, int) and t < 2):
                    ve.wait_ge(s_yc, t - 1)
                ve.reduce_sum(slot_p[:, b, :], slot_pe[:, :, :], AX_X).then_inc(s_ps, 1)

            def scale_y(t, n, b, first):
                ve.wait_ge(s_y, t + 1)
                ve.wait_ge(s_ps, t + 1)
                if not first:
                    ve.wait_ge(s_ys[b], n * 16)
                ve.tensor_tensor(yo[b].rearrange("p (j d) -> p j d", j=GT),
                                 PD[:, 512:1024].rearrange("p (j d) -> p j d", j=GT),
                                 slot_p[:, b, :].unsqueeze(2).broadcast_to([P, GT, D]), ALU.mult).then_inc(s_yc, 1)

            def tile_step_v(t, n, b, early=False, last=False):
                glu(t, b, early)
                if not last:
                    low(t + 1, 1 - b, early and t == 0)
                    own_p(t + 1, n + b, 1 - b)
                if not (early and t == 0):
                    scale_y(t - 1, n + b - 1, 1 - b, early or (isinstance(t, int) and t < 3))
                if not last:
                    sum_p(t + 1, 1 - b)

            def back(k):
                link(ve.tensor_tensor(L2, chosen[:, k], move.unsqueeze(1).broadcast_to([P, TILES, EXPERTS]), ALU.mult))
                link(ve.reduce_sum(c1, L2, AX_X))
                link(ve.tensor_tensor(sf[:, k, :], sf[:, k, :], c1, ALU.add))
                ve.tensor_copy(back_u[:, k, :], sf[:, k, :]).then_inc(s_back, 1)

            own_p(0, 0, 0)
            sum_p(0, 0)
            held = STEPS_A - 1
            low(0, 0, True)
            chain(held, held % SLOT3, 1)
            for t in range(2):
                tile_step_v(t, t // 2, t % 2, early=True)
                chain(held, held % SLOT3, 2 + t)
            tile_step_v(2, 1, 0)
            chain(held, held % SLOT3, 4)
            with ve.Fori(0, (MOE_TILES - 5) // 2) as i:
                tile_step_v(i * 2 + 3, i + 1, 1)
                tile_step_v(i * 2 + 4, i + 2, 0)
            back(0)
            tile_step_v(MOE_TILES - 2, (MOE_TILES - 2) // 2, 1)
            back(1)
            ve.wait_ge(s_back, TOP_K)
            tile_step_v(MOE_TILES - 1, (MOE_TILES - 1) // 2, 0, last=True)
            scale_y(MOE_TILES - 1, (MOE_TILES - 1) // 2, 0, False)

            mixer(ve, mix, STEPS_A, GROUPS + 2)


_INS = ['L0_attn_x', 'L0_attn_W_in', 'L0_attn_conv_w', 'L0_attn_conv_b', 'L0_attn_W_x', 'L0_attn_W_dt',
        'L0_attn_b_dt', 'L0_attn_A_log', 'L0_attn_D', 'L0_attn_W_out', 'L0_ffn_w_gate', 'L0_ffn_w1',
        'L0_ffn_w3', 'L0_ffn_w2']
_OUTS = [((BATCH, SEQ, D), 'float32')]


def kernel(**inputs):
    import numpy as _np
    import concourse.bacc as _bacc
    from concourse import mybir as _mybir
    from concourse.bass_utils import run_bass_kernel_spmd as _run

    nc = _bacc.Bacc("TRN2", target_bir_lowering=False, num_devices=1)
    arrays, args = {}, []
    for name in _INS:
        a = _np.ascontiguousarray(inputs[name])
        arrays[f"in_{name}_dram"] = a
        args.append(nc.dram_tensor(f"in_{name}_dram", a.shape, _mybir.dt.from_np(a.dtype), kind="ExternalInput").ap())
    for i, (shape, dtype) in enumerate(_OUTS):
        dt = _mybir.dt.from_np(_np.dtype(dtype))
        args.append(nc.dram_tensor(f"out_{i}_dram", shape, dt, kind="ExternalOutput").ap())
    block_kernel(nc, *args)
    r = _run(nc, [arrays], core_ids=[0])
    return r.results[0]["out_0_dram"]
```
